# Optimizing a Trainium2 kernel written in Bass

```python
import numpy as np
import jax
import jax.numpy as jnp

def _softmax(x, axis=-1):
    return jax.nn.softmax(x, axis=axis)

def _gelu(x):
    return jax.nn.gelu(x, approximate=True)

def _silu(x):
    return jax.nn.silu(x)

def _sigmoid(x):
    return jax.nn.sigmoid(x)

def _layernorm(x, axis=-1, eps=1e-05):
    m = jnp.mean(x, axis=axis, keepdims=True)
    v = jnp.var(x, axis=axis, keepdims=True)
    return (x - m) / jnp.sqrt(v + eps)

def _scatter_add(tgt, idx, src, axis=0):
    return tgt.at[idx].add(src)

def _segment_sum(src, seg, n):
    return jax.ops.segment_sum(src, seg, n)
kernel_name = 'mk_rec_standalone_d1_rec_r8_17aa39'

def setup_inputs(seed: int=0):
    np.random.seed(seed)
    _w = jnp.asarray

    def _rec_inputs():
        import jax
        import jax.numpy as jnp
        _rk = jax.random.key(seed)
        r_seq = jnp.stack([jax.random.randint(jax.random.fold_in(jax.random.fold_in(_rk, 1), 0), (512,), 171, 99919, jnp.int32), jax.random.randint(jax.random.fold_in(jax.random.fold_in(_rk, 1), 1), (512,), 77, 99188, jnp.int32), jax.random.randint(jax.random.fold_in(jax.random.fold_in(_rk, 1), 2), (512,), 29, 99986, jnp.int32), jax.random.randint(jax.random.fold_in(jax.random.fold_in(_rk, 1), 3), (512,), 67, 99858, jnp.int32), jax.random.randint(jax.random.fold_in(jax.random.fold_in(_rk, 1), 4), (512,), 68, 99700, jnp.int32), jax.random.randint(jax.random.fold_in(jax.random.fold_in(_rk, 1), 5), (512,), 167, 99906, jnp.int32), jax.random.randint(jax.random.fold_in(jax.random.fold_in(_rk, 1), 6), (512,), 161, 99745, jnp.int32), jax.random.randint(jax.random.fold_in(jax.random.fold_in(_rk, 1), 7), (512,), 113, 99925, jnp.int32), jax.random.randint(jax.random.fold_in(jax.random.fold_in(_rk, 1), 8), (512,), 114, 12425, jnp.int32), jax.random.randint(jax.random.fold_in(jax.random.fold_in(_rk, 1), 9), (512,), 13, 12454, jnp.int32), jax.random.randint(jax.random.fold_in(jax.random.fold_in(_rk, 1), 10), (512,), 387, 99701, jnp.int32), jax.random.randint(jax.random.fold_in(jax.random.fold_in(_rk, 1), 11), (512,), 146, 12431, jnp.int32), jax.random.randint(jax.random.fold_in(jax.random.fold_in(_rk, 1), 12), (512,), 80, 12467, jnp.int32), jax.random.randint(jax.random.fold_in(jax.random.fold_in(_rk, 1), 13), (512,), 455, 99555, jnp.int32), jax.random.randint(jax.random.fold_in(jax.random.fold_in(_rk, 1), 14), (512,), 182, 99892, jnp.int32), jax.random.randint(jax.random.fold_in(jax.random.fold_in(_rk, 1), 15), (512,), 159, 99939, jnp.int32), jax.random.randint(jax.random.fold_in(jax.random.fold_in(_rk, 1), 16), (512,), 28, 99865, jnp.int32), jax.random.randint(jax.random.fold_in(jax.random.fold_in(_rk, 1), 17), (512,), 90, 99935, jnp.int32), jax.random.randint(jax.random.fold_in(jax.random.fold_in(_rk, 1), 18), (512,), 86, 99796, jnp.int32), jax.random.randint(jax.random.fold_in(jax.random.fold_in(_rk, 1), 19), (512,), 18, 12488, jnp.int32), jax.random.randint(jax.random.fold_in(jax.random.fold_in(_rk, 1), 20), (512,), 78, 99909, jnp.int32), jax.random.randint(jax.random.fold_in(jax.random.fold_in(_rk, 1), 21), (512,), 131, 99946, jnp.int32), jax.random.randint(jax.random.fold_in(jax.random.fold_in(_rk, 1), 22), (512,), 264, 99913, jnp.int32), jax.random.randint(jax.random.fold_in(jax.random.fold_in(_rk, 1), 23), (512,), 203, 99844, jnp.int32), jax.random.randint(jax.random.fold_in(jax.random.fold_in(_rk, 1), 24), (512,), 126, 99953, jnp.int32), jax.random.randint(jax.random.fold_in(jax.random.fold_in(_rk, 1), 25), (512,), 90, 99942, jnp.int32), jax.random.randint(jax.random.fold_in(jax.random.fold_in(_rk, 1), 26), (512,), 163, 99823, jnp.int32), jax.random.randint(jax.random.fold_in(jax.random.fold_in(_rk, 1), 27), (512,), 104, 99938, jnp.int32), jax.random.randint(jax.random.fold_in(jax.random.fold_in(_rk, 1), 28), (512,), 138, 99972, jnp.int32), jax.random.randint(jax.random.fold_in(jax.random.fold_in(_rk, 1), 29), (512,), 190, 99946, jnp.int32), jax.random.randint(jax.random.fold_in(jax.random.fold_in(_rk, 1), 30), (512,), 394, 99874, jnp.int32), jax.random.randint(jax.random.fold_in(jax.random.fold_in(_rk, 1), 31), (512,), 192, 99871, jnp.int32), jax.random.randint(jax.random.fold_in(jax.random.fold_in(_rk, 1), 32), (512,), 100, 99909, jnp.int32), jax.random.randint(jax.random.fold_in(jax.random.fold_in(_rk, 1), 33), (512,), 47, 99778, jnp.int32), jax.random.randint(jax.random.fold_in(jax.random.fold_in(_rk, 1), 34), (512,), 262, 99945, jnp.int32), jax.random.randint(jax.random.fold_in(jax.random.fold_in(_rk, 1), 35), (512,), 60, 99998, jnp.int32), jax.random.randint(jax.random.fold_in(jax.random.fold_in(_rk, 1), 36), (512,), 302, 99923, jnp.int32), jax.random.randint(jax.random.fold_in(jax.random.fold_in(_rk, 1), 37), (512,), 54, 99906, jnp.int32), jax.random.randint(jax.random.fold_in(jax.random.fold_in(_rk, 1), 38), (512,), 144, 99955, jnp.int32), jax.random.randint(jax.random.fold_in(jax.random.fold_in(_rk, 1), 39), (512,), 14, 99839, jnp.int32), jax.random.randint(jax.random.fold_in(jax.random.fold_in(_rk, 1), 40), (512,), 171, 99738, jnp.int32), jax.random.randint(jax.random.fold_in(jax.random.fold_in(_rk, 1), 41), (512,), 33, 12464, jnp.int32), jax.random.randint(jax.random.fold_in(jax.random.fold_in(_rk, 1), 42), (512,), 51, 99990, jnp.int32), jax.random.randint(jax.random.fold_in(jax.random.fold_in(_rk, 1), 43), (512,), 45, 99982, jnp.int32), jax.random.randint(jax.random.fold_in(jax.random.fold_in(_rk, 1), 44), (512,), 86, 99940, jnp.int32), jax.random.randint(jax.random.fold_in(jax.random.fold_in(_rk, 1), 45), (512,), 263, 99699, jnp.int32), jax.random.randint(jax.random.fold_in(jax.random.fold_in(_rk, 1), 46), (512,), 300, 99582, jnp.int32), jax.random.randint(jax.random.fold_in(jax.random.fold_in(_rk, 1), 47), (512,), 95, 12494, jnp.int32), jax.random.randint(jax.random.fold_in(jax.random.fold_in(_rk, 1), 48), (512,), 156, 99964, jnp.int32), jax.random.randint(jax.random.fold_in(jax.random.fold_in(_rk, 1), 49), (512,), 145, 99578, jnp.int32), jax.random.randint(jax.random.fold_in(jax.random.fold_in(_rk, 1), 50), (512,), 433, 99602, jnp.int32), jax.random.randint(jax.random.fold_in(jax.random.fold_in(_rk, 1), 51), (512,), 252, 12494, jnp.int32), jax.random.randint(jax.random.fold_in(jax.random.fold_in(_rk, 1), 52), (512,), 281, 99727, jnp.int32), jax.random.randint(jax.random.fold_in(jax.random.fold_in(_rk, 1), 53), (512,), 347, 12476, jnp.int32), jax.random.randint(jax.random.fold_in(jax.random.fold_in(_rk, 1), 54), (512,), 875, 99948, jnp.int32), jax.random.randint(jax.random.fold_in(jax.random.fold_in(_rk, 1), 55), (512,), 83, 99942, jnp.int32), jax.random.randint(jax.random.fold_in(jax.random.fold_in(_rk, 1), 56), (512,), 1, 99971, jnp.int32), jax.random.randint(jax.random.fold_in(jax.random.fold_in(_rk, 1), 57), (512,), 31, 99986, jnp.int32), jax.random.randint(jax.random.fold_in(jax.random.fold_in(_rk, 1), 58), (512,), 128, 99996, jnp.int32), jax.random.randint(jax.random.fold_in(jax.random.fold_in(_rk, 1), 59), (512,), 72, 99817, jnp.int32), jax.random.randint(jax.random.fold_in(jax.random.fold_in(_rk, 1), 60), (512,), 127, 99745, jnp.int32), jax.random.randint(jax.random.fold_in(jax.random.fold_in(_rk, 1), 61), (512,), 181, 99797, jnp.int32), jax.random.randint(jax.random.fold_in(jax.random.fold_in(_rk, 1), 62), (512,), 231, 12480, jnp.int32), jax.random.randint(jax.random.fold_in(jax.random.fold_in(_rk, 1), 63), (512,), 96, 99973, jnp.int32), jax.random.randint(jax.random.fold_in(jax.random.fold_in(_rk, 1), 64), (512,), 51, 99950, jnp.int32), jax.random.randint(jax.random.fold_in(jax.random.fold_in(_rk, 1), 65), (512,), 42, 99755, jnp.int32), jax.random.randint(jax.random.fold_in(jax.random.fold_in(_rk, 1), 66), (512,), 553, 99291, jnp.int32), jax.random.randint(jax.random.fold_in(jax.random.fold_in(_rk, 1), 67), (512,), 20, 99962, jnp.int32), jax.random.randint(jax.random.fold_in(jax.random.fold_in(_rk, 1), 68), (512,), 11, 99506, jnp.int32), jax.random.randint(jax.random.fold_in(jax.random.fold_in(_rk, 1), 69), (512,), 121, 99714, jnp.int32), jax.random.randint(jax.random.fold_in(jax.random.fold_in(_rk, 1), 70), (512,), 250, 99746, jnp.int32), jax.random.randint(jax.random.fold_in(jax.random.fold_in(_rk, 1), 71), (512,), 325, 99862, jnp.int32), jax.random.randint(jax.random.fold_in(jax.random.fold_in(_rk, 1), 72), (512,), 129, 99466, jnp.int32), jax.random.randint(jax.random.fold_in(jax.random.fold_in(_rk, 1), 73), (512,), 372, 99861, jnp.int32), jax.random.randint(jax.random.fold_in(jax.random.fold_in(_rk, 1), 74), (512,), 5, 12487, jnp.int32), jax.random.randint(jax.random.fold_in(jax.random.fold_in(_rk, 1), 75), (512,), 193, 12459, jnp.int32), jax.random.randint(jax.random.fold_in(jax.random.fold_in(_rk, 1), 76), (512,), 492, 99911, jnp.int32), jax.random.randint(jax.random.fold_in(jax.random.fold_in(_rk, 1), 77), (512,), 15, 12482, jnp.int32), jax.random.randint(jax.random.fold_in(jax.random.fold_in(_rk, 1), 78), (512,), 44, 99993, jnp.int32), jax.random.randint(jax.random.fold_in(jax.random.fold_in(_rk, 1), 79), (512,), 53, 99881, jnp.int32), jax.random.randint(jax.random.fold_in(jax.random.fold_in(_rk, 1), 80), (512,), 786, 99754, jnp.int32), jax.random.randint(jax.random.fold_in(jax.random.fold_in(_rk, 1), 81), (512,), 116, 99810, jnp.int32), jax.random.randint(jax.random.fold_in(jax.random.fold_in(_rk, 1), 82), (512,), 212, 99535, jnp.int32), jax.random.randint(jax.random.fold_in(jax.random.fold_in(_rk, 1), 83), (512,), 325, 99866, jnp.int32), jax.random.randint(jax.random.fold_in(jax.random.fold_in(_rk, 1), 84), (512,), 171, 99660, jnp.int32), jax.random.randint(jax.random.fold_in(jax.random.fold_in(_rk, 1), 85), (512,), 19, 99949, jnp.int32), jax.random.randint(jax.random.fold_in(jax.random.fold_in(_rk, 1), 86), (512,), 148, 99807, jnp.int32), jax.random.randint(jax.random.fold_in(jax.random.fold_in(_rk, 1), 87), (512,), 68, 99893, jnp.int32), jax.random.randint(jax.random.fold_in(jax.random.fold_in(_rk, 1), 88), (512,), 53, 99881, jnp.int32), jax.random.randint(jax.random.fold_in(jax.random.fold_in(_rk, 1), 89), (512,), 921, 99531, jnp.int32), jax.random.randint(jax.random.fold_in(jax.random.fold_in(_rk, 1), 90), (512,), 276, 99937, jnp.int32), jax.random.randint(jax.random.fold_in(jax.random.fold_in(_rk, 1), 91), (512,), 1, 99514, jnp.int32), jax.random.randint(jax.random.fold_in(jax.random.fold_in(_rk, 1), 92), (512,), 103, 99847, jnp.int32), jax.random.randint(jax.random.fold_in(jax.random.fold_in(_rk, 1), 93), (512,), 329, 99980, jnp.int32), jax.random.randint(jax.random.fold_in(jax.random.fold_in(_rk, 1), 94), (512,), 185, 99967, jnp.int32), jax.random.randint(jax.random.fold_in(jax.random.fold_in(_rk, 1), 95), (512,), 294, 99626, jnp.int32), jax.random.randint(jax.random.fold_in(jax.random.fold_in(_rk, 1), 96), (512,), 215, 99847, jnp.int32), jax.random.randint(jax.random.fold_in(jax.random.fold_in(_rk, 1), 97), (512,), 11, 99516, jnp.int32), jax.random.randint(jax.random.fold_in(jax.random.fold_in(_rk, 1), 98), (512,), 671, 12494, jnp.int32), jax.random.randint(jax.random.fold_in(jax.random.fold_in(_rk, 1), 99), (512,), 178, 99919, jnp.int32), jax.random.randint(jax.random.fold_in(jax.random.fold_in(_rk, 1), 100), (512,), 76, 99975, jnp.int32), jax.random.randint(jax.random.fold_in(jax.random.fold_in(_rk, 1), 101), (512,), 55, 99501, jnp.int32), jax.random.randint(jax.random.fold_in(jax.random.fold_in(_rk, 1), 102), (512,), 92, 99778, jnp.int32), jax.random.randint(jax.random.fold_in(jax.random.fold_in(_rk, 1), 103), (512,), 417, 99987, jnp.int32), jax.random.randint(jax.random.fold_in(jax.random.fold_in(_rk, 1), 104), (512,), 28, 99965, jnp.int32), jax.random.randint(jax.random.fold_in(jax.random.fold_in(_rk, 1), 105), (512,), 36, 99663, jnp.int32), jax.random.randint(jax.random.fold_in(jax.random.fold_in(_rk, 1), 106), (512,), 624, 99965, jnp.int32), jax.random.randint(jax.random.fold_in(jax.random.fold_in(_rk, 1), 107), (512,), 45, 99945, jnp.int32), jax.random.randint(jax.random.fold_in(jax.random.fold_in(_rk, 1), 108), (512,), 36, 99951, jnp.int32), jax.random.randint(jax.random.fold_in(jax.random.fold_in(_rk, 1), 109), (512,), 15, 99854, jnp.int32), jax.random.randint(jax.random.fold_in(jax.random.fold_in(_rk, 1), 110), (512,), 39, 99839, jnp.int32), jax.random.randint(jax.random.fold_in(jax.random.fold_in(_rk, 1), 111), (512,), 409, 99964, jnp.int32), jax.random.randint(jax.random.fold_in(jax.random.fold_in(_rk, 1), 112), (512,), 39, 99990, jnp.int32), jax.random.randint(jax.random.fold_in(jax.random.fold_in(_rk, 1), 113), (512,), 467, 99821, jnp.int32), jax.random.randint(jax.random.fold_in(jax.random.fold_in(_rk, 1), 114), (512,), 364, 99626, jnp.int32), jax.random.randint(jax.random.fold_in(jax.random.fold_in(_rk, 1), 115), (512,), 207, 99917, jnp.int32), jax.random.randint(jax.random.fold_in(jax.random.fold_in(_rk, 1), 116), (512,), 259, 99729, jnp.int32), jax.random.randint(jax.random.fold_in(jax.random.fold_in(_rk, 1), 117), (512,), 28, 99988, jnp.int32), jax.random.randint(jax.random.fold_in(jax.random.fold_in(_rk, 1), 118), (512,), 7, 99909, jnp.int32), jax.random.randint(jax.random.fold_in(jax.random.fold_in(_rk, 1), 119), (512,), 159, 12488, jnp.int32), jax.random.randint(jax.random.fold_in(jax.random.fold_in(_rk, 1), 120), (512,), 17, 99900, jnp.int32), jax.random.randint(jax.random.fold_in(jax.random.fold_in(_rk, 1), 121), (512,), 231, 99987, jnp.int32), jax.random.randint(jax.random.fold_in(jax.random.fold_in(_rk, 1), 122), (512,), 282, 99501, jnp.int32), jax.random.randint(jax.random.fold_in(jax.random.fold_in(_rk, 1), 123), (512,), 32, 99652, jnp.int32), jax.random.randint(jax.random.fold_in(jax.random.fold_in(_rk, 1), 124), (512,), 78, 99494, jnp.int32), jax.random.randint(jax.random.fold_in(jax.random.fold_in(_rk, 1), 125), (512,), 418, 99629, jnp.int32), jax.random.randint(jax.random.fold_in(jax.random.fold_in(_rk, 1), 126), (512,), 98, 99843, jnp.int32), jax.random.randint(jax.random.fold_in(jax.random.fold_in(_rk, 1), 127), (512,), 350, 99447, jnp.int32), jax.random.randint(jax.random.fold_in(jax.random.fold_in(_rk, 1), 128), (512,), 42, 99778, jnp.int32), jax.random.randint(jax.random.fold_in(jax.random.fold_in(_rk, 1), 129), (512,), 431, 99743, jnp.int32), jax.random.randint(jax.random.fold_in(jax.random.fold_in(_rk, 1), 130), (512,), 118, 99903, jnp.int32), jax.random.randint(jax.random.fold_in(jax.random.fold_in(_rk, 1), 131), (512,), 194, 99794, jnp.int32), jax.random.randint(jax.random.fold_in(jax.random.fold_in(_rk, 1), 132), (512,), 22, 99954, jnp.int32), jax.random.randint(jax.random.fold_in(jax.random.fold_in(_rk, 1), 133), (512,), 17, 99770, jnp.int32), jax.random.randint(jax.random.fold_in(jax.random.fold_in(_rk, 1), 134), (512,), 46, 99855, jnp.int32), jax.random.randint(jax.random.fold_in(jax.random.fold_in(_rk, 1), 135), (512,), 804, 99713, jnp.int32), jax.random.randint(jax.random.fold_in(jax.random.fold_in(_rk, 1), 136), (512,), 593, 99653, jnp.int32), jax.random.randint(jax.random.fold_in(jax.random.fold_in(_rk, 1), 137), (512,), 123, 12487, jnp.int32), jax.random.randint(jax.random.fold_in(jax.random.fold_in(_rk, 1), 138), (512,), 193, 99684, jnp.int32), jax.random.randint(jax.random.fold_in(jax.random.fold_in(_rk, 1), 139), (512,), 655, 99978, jnp.int32), jax.random.randint(jax.random.fold_in(jax.random.fold_in(_rk, 1), 140), (512,), 405, 99969, jnp.int32), jax.random.randint(jax.random.fold_in(jax.random.fold_in(_rk, 1), 141), (512,), 92, 99884, jnp.int32), jax.random.randint(jax.random.fold_in(jax.random.fold_in(_rk, 1), 142), (512,), 169, 99691, jnp.int32), jax.random.randint(jax.random.fold_in(jax.random.fold_in(_rk, 1), 143), (512,), 396, 12487, jnp.int32), jax.random.randint(jax.random.fold_in(jax.random.fold_in(_rk, 1), 144), (512,), 5, 99706, jnp.int32), jax.random.randint(jax.random.fold_in(jax.random.fold_in(_rk, 1), 145), (512,), 270, 99879, jnp.int32), jax.random.randint(jax.random.fold_in(jax.random.fold_in(_rk, 1), 146), (512,), 142, 99894, jnp.int32), jax.random.randint(jax.random.fold_in(jax.random.fold_in(_rk, 1), 147), (512,), 62, 99921, jnp.int32), jax.random.randint(jax.random.fold_in(jax.random.fold_in(_rk, 1), 148), (512,), 3, 99767, jnp.int32), jax.random.randint(jax.random.fold_in(jax.random.fold_in(_rk, 1), 149), (512,), 162, 99523, jnp.int32), jax.random.randint(jax.random.fold_in(jax.random.fold_in(_rk, 1), 150), (512,), 158, 99917, jnp.int32), jax.random.randint(jax.random.fold_in(jax.random.fold_in(_rk, 1), 151), (512,), 276, 99790, jnp.int32), jax.random.randint(jax.random.fold_in(jax.random.fold_in(_rk, 1), 152), (512,), 168, 99818, jnp.int32), jax.random.randint(jax.random.fold_in(jax.random.fold_in(_rk, 1), 153), (512,), 862, 99057, jnp.int32), jax.random.randint(jax.random.fold_in(jax.random.fold_in(_rk, 1), 154), (512,), 226, 99887, jnp.int32), jax.random.randint(jax.random.fold_in(jax.random.fold_in(_rk, 1), 155), (512,), 176, 99988, jnp.int32), jax.random.randint(jax.random.fold_in(jax.random.fold_in(_rk, 1), 156), (512,), 153, 12479, jnp.int32), jax.random.randint(jax.random.fold_in(jax.random.fold_in(_rk, 1), 157), (512,), 208, 99870, jnp.int32), jax.random.randint(jax.random.fold_in(jax.random.fold_in(_rk, 1), 158), (512,), 95, 99483, jnp.int32), jax.random.randint(jax.random.fold_in(jax.random.fold_in(_rk, 1), 159), (512,), 180, 12482, jnp.int32), jax.random.randint(jax.random.fold_in(jax.random.fold_in(_rk, 1), 160), (512,), 603, 12488, jnp.int32), jax.random.randint(jax.random.fold_in(jax.random.fold_in(_rk, 1), 161), (512,), 231, 12473, jnp.int32), jax.random.randint(jax.random.fold_in(jax.random.fold_in(_rk, 1), 162), (512,), 28, 12454, jnp.int32), jax.random.randint(jax.random.fold_in(jax.random.fold_in(_rk, 1), 163), (512,), 6, 99860, jnp.int32), jax.random.randint(jax.random.fold_in(jax.random.fold_in(_rk, 1), 164), (512,), 15, 99886, jnp.int32), jax.random.randint(jax.random.fold_in(jax.random.fold_in(_rk, 1), 165), (512,), 131, 99907, jnp.int32), jax.random.randint(jax.random.fold_in(jax.random.fold_in(_rk, 1), 166), (512,), 400, 99988, jnp.int32), jax.random.randint(jax.random.fold_in(jax.random.fold_in(_rk, 1), 167), (512,), 10, 99687, jnp.int32), jax.random.randint(jax.random.fold_in(jax.random.fold_in(_rk, 1), 168), (512,), 58, 99998, jnp.int32), jax.random.randint(jax.random.fold_in(jax.random.fold_in(_rk, 1), 169), (512,), 260, 99957, jnp.int32), jax.random.randint(jax.random.fold_in(jax.random.fold_in(_rk, 1), 170), (512,), 81, 99987, jnp.int32), jax.random.randint(jax.random.fold_in(jax.random.fold_in(_rk, 1), 171), (512,), 163, 99770, jnp.int32), jax.random.randint(jax.random.fold_in(jax.random.fold_in(_rk, 1), 172), (512,), 122, 99962, jnp.int32), jax.random.randint(jax.random.fold_in(jax.random.fold_in(_rk, 1), 173), (512,), 64, 99883, jnp.int32), jax.random.randint(jax.random.fold_in(jax.random.fold_in(_rk, 1), 174), (512,), 275, 99877, jnp.int32), jax.random.randint(jax.random.fold_in(jax.random.fold_in(_rk, 1), 175), (512,), 10, 99705, jnp.int32), jax.random.randint(jax.random.fold_in(jax.random.fold_in(_rk, 1), 176), (512,), 262, 99986, jnp.int32), jax.random.randint(jax.random.fold_in(jax.random.fold_in(_rk, 1), 177), (512,), 164, 99805, jnp.int32), jax.random.randint(jax.random.fold_in(jax.random.fold_in(_rk, 1), 178), (512,), 277, 99725, jnp.int32), jax.random.randint(jax.random.fold_in(jax.random.fold_in(_rk, 1), 179), (512,), 185, 99473, jnp.int32), jax.random.randint(jax.random.fold_in(jax.random.fold_in(_rk, 1), 180), (512,), 35, 99962, jnp.int32), jax.random.randint(jax.random.fold_in(jax.random.fold_in(_rk, 1), 181), (512,), 282, 99963, jnp.int32), jax.random.randint(jax.random.fold_in(jax.random.fold_in(_rk, 1), 182), (512,), 225, 99926, jnp.int32), jax.random.randint(jax.random.fold_in(jax.random.fold_in(_rk, 1), 183), (512,), 65, 99946, jnp.int32), jax.random.randint(jax.random.fold_in(jax.random.fold_in(_rk, 1), 184), (512,), 119, 99892, jnp.int32), jax.random.randint(jax.random.fold_in(jax.random.fold_in(_rk, 1), 185), (512,), 177, 99866, jnp.int32), jax.random.randint(jax.random.fold_in(jax.random.fold_in(_rk, 1), 186), (512,), 24, 99790, jnp.int32), jax.random.randint(jax.random.fold_in(jax.random.fold_in(_rk, 1), 187), (512,), 131, 99684, jnp.int32), jax.random.randint(jax.random.fold_in(jax.random.fold_in(_rk, 1), 188), (512,), 114, 99613, jnp.int32), jax.random.randint(jax.random.fold_in(jax.random.fold_in(_rk, 1), 189), (512,), 180, 99991, jnp.int32), jax.random.randint(jax.random.fold_in(jax.random.fold_in(_rk, 1), 190), (512,), 88, 99788, jnp.int32), jax.random.randint(jax.random.fold_in(jax.random.fold_in(_rk, 1), 191), (512,), 14, 12487, jnp.int32), jax.random.randint(jax.random.fold_in(jax.random.fold_in(_rk, 1), 192), (512,), 79, 12471, jnp.int32), jax.random.randint(jax.random.fold_in(jax.random.fold_in(_rk, 1), 193), (512,), 229, 99942, jnp.int32), jax.random.randint(jax.random.fold_in(jax.random.fold_in(_rk, 1), 194), (512,), 52, 99879, jnp.int32), jax.random.randint(jax.random.fold_in(jax.random.fold_in(_rk, 1), 195), (512,), 61, 99977, jnp.int32), jax.random.randint(jax.random.fold_in(jax.random.fold_in(_rk, 1), 196), (512,), 476, 99809, jnp.int32), jax.random.randint(jax.random.fold_in(jax.random.fold_in(_rk, 1), 197), (512,), 91, 99425, jnp.int32), jax.random.randint(jax.random.fold_in(jax.random.fold_in(_rk, 1), 198), (512,), 252, 12474, jnp.int32), jax.random.randint(jax.random.fold_in(jax.random.fold_in(_rk, 1), 199), (512,), 49, 99873, jnp.int32)], axis=1)
        return r_seq
    r_seq = _rec_inputs()

    def _L0_rec_setup():
        import jax, jax.numpy as jnp
        import numpy as np
        N_ITEMS = 12500
        HIDDEN = 128
        SEQ = 200
        K = 4
        ITERS = 3
        POW = 1.0
        BATCH = 512

        def squash(s):
            n = jnp.linalg.norm(s, axis=-1, keepdims=True)
            n2 = n * n
            return n2 / (1.0 + n2) * (s / (n + 1e-12))
        key = jax.random.key(seed)
        k1, k2, k3, k4 = jax.random.split(key, 4)
        seq = jax.random.randint(k1, (BATCH, SEQ), 0, N_ITEMS)
        emb_table = jax.random.normal(k2, (N_ITEMS, HIDDEN), dtype=jnp.float32) * 0.02
        emb_table = emb_table.at[0].set(0.0)
        bound = 1.0 / np.sqrt(HIDDEN)
        s_w = jax.random.uniform(k3, (HIDDEN, HIDDEN * K), dtype=jnp.float32, minval=-bound, maxval=bound)
        s_b = jax.random.uniform(k4, (HIDDEN * K,), dtype=jnp.float32, minval=-bound, maxval=bound)
        return {'seq': seq, 'emb_table': emb_table, 's_w': s_w, 's_b': s_b}
    _L0_rec_all = _L0_rec_setup()
    _L0_rec_in = {k: v for k, v in _L0_rec_all.items() if k in ('emb_table', 's_w', 's_b')}
    del _L0_rec_all
    return {'r_seq': r_seq, 'L0_rec_emb_table': _L0_rec_in['emb_table'], 'L0_rec_s_w': _L0_rec_in['s_w'], 'L0_rec_s_b': _L0_rec_in['s_b']}

def reference(r_seq, L0_rec_emb_table, L0_rec_s_w, L0_rec_s_b):
    import jax
    import jax.numpy as jnp

    def _L0_rec_ref(seq, emb_table, s_w, s_b):
        import jax, jax.numpy as jnp
        import numpy as np
        N_ITEMS = 12500
        HIDDEN = 128
        SEQ = 200
        K = 4
        ITERS = 3
        POW = 1.0
        BATCH = 512

        def squash(s):
            n = jnp.linalg.norm(s, axis=-1, keepdims=True)
            n2 = n * n
            return n2 / (1.0 + n2) * (s / (n + 1e-12))
        mask = (seq != 0).astype(jnp.float32)
        lut = emb_table.at[0].set(jax.lax.stop_gradient(emb_table[0]))
        item_emb = lut[seq]
        u = item_emb @ s_w + s_b
        b, s = seq.shape
        u = u.reshape(b, s, K, HIDDEN).transpose(0, 2, 1, 3)
        u = jax.lax.stop_gradient(u)
        m = mask[:, None, :]
        capsule_b = jnp.zeros((b, K, s), dtype=jnp.float32)
        v = None
        for _ in range(ITERS):
            capsule_b = jnp.where(m == 0, -10000.0, capsule_b)
            c = jax.nn.softmax(capsule_b, axis=1)
            sv = jnp.einsum('bks,bksd->bkd', c, u)
            v = squash(sv)
            capsule_b = capsule_b + jnp.einsum('bksd,bkd->bks', u, v)
        interest = v
        last_item = lut[seq[:, -1]]
        att = jnp.einsum('bd,bkd->bk', last_item, interest)
        att = att ** POW
        w = jax.nn.softmax(att, axis=-1)
        final = jnp.einsum('bk,bkd->bd', w, interest)
        score = final @ emb_table.T
        return score
    y = _L0_rec_ref(r_seq, L0_rec_emb_table, L0_rec_s_w, L0_rec_s_b)
    return y

_drawn_inputs = setup_inputs


def setup_inputs(seed=0):
    import zlib

    import numpy as np

    out = dict(_drawn_inputs(seed))
    spreads = {}
    factors = {}
    for name, (base, spread) in spreads.items():
        noise = np.random.default_rng([zlib.crc32(name.encode()), seed]).standard_normal(out[name].shape)
        drawn = base * np.exp(spread * noise) if base else spread * noise
        out[name] = jnp.asarray(drawn.astype(out[name].dtype))
    for name, factor in factors.items():
        out[name] = (out[name] * factor).astype(out[name].dtype)
    return out
```

```python
from contextlib import ExitStack

import concourse.bass as bass
from concourse import mybir

F32 = mybir.dt.float32
I32 = mybir.dt.int32
ALU = mybir.AluOpType
ACT = mybir.ActivationFunctionType
AX = mybir.AxisListType.X

P = 128
STEPS = 3


def capsule_routing(nc, r_seq, table, s_w, s_b, out):
    BATCH, SEQ = r_seq.shape
    ITEMS, D = table.shape
    K = s_w.shape[1] // D
    assert D == P and BATCH % P == 0 and s_b.shape[0] == K * D
    CHUNKS = BATCH // P
    SLOTS = 64
    HALVES = P // SLOTS
    TILES = P // HALVES
    PAIRS = TILES * HALVES
    COLS = PAIRS * K
    BLOCK = 8
    BLOCKS = TILES // BLOCK
    FILL = 4
    GONE = -30000.0
    EPS = 1e-12
    TINY = 1e-30

    GROUP = FILL * P
    GROUPS = -(-ITEMS // GROUP)
    STAGES = 8
    UNIT = 500
    UNITS = ITEMS // UNIT
    assert UNITS * UNIT == ITEMS
    STORE = 5
    STORES = UNITS // STORE
    GAPS = [7, 4, 6, 4, 4]
    assert sum(GAPS) == UNITS and STORES * STORE == UNITS

    def group_parts(g):
        return min(GROUP, ITEMS - g * GROUP) // FILL

    assert all(group_parts(g) * FILL == min(GROUP, ITEMS - g * GROUP) for g in range(GROUPS))

    def table_fills(block):
        lead = GROUPS - 3 * BLOCKS
        return range(0, 4 + lead) if block < 0 else range(
            min(GROUPS, 4 + lead + 3 * block), min(GROUPS, 4 + lead + 3 * (block + 1)))

    fills = [("table", g) for g in table_fills(-1)]
    for c in range(CHUNKS):
        for blk in range(BLOCKS):
            fills += [("items", c, blk * (BLOCK // FILL) + q) for q in range(BLOCK // FILL)]
            if c == 0:
                fills += [("table", g) for g in table_fills(blk)]
    fill_at = {f: n for n, f in enumerate(fills)}
    assert len(fills) == GROUPS + CHUNKS * TILES // FILL
    last_table_fill = fill_at[("table", GROUPS - 1)]

    ctx = ExitStack()
    with ctx:
        def sb(name, shape, dt=F32):
            return ctx.enter_context(nc.sbuf_tensor(name, shape, dt))

        def bank(name):
            return ctx.enter_context(nc.psum_tensor(name, [P, 512], F32))

        def sem(name):
            return ctx.enter_context(nc.semaphore(name))

        tableT = sb("tableT", [P, ITEMS])
        rows = [sb(f"rows{i}", [P, TILES * D]) for i in range(2)]
        rowsT = sb("rowsT", [P, TILES * P])
        outst = sb("outst", [P, 2, STORE * UNIT])
        stage = rows[1]
        w = sb("w", [P, K * D])
        wT = sb("wT", [P, K * D])
        bias_col = sb("bias_col", [P, K])
        bias_all = sb("bias_all", [P, K * D])
        bias_rep = sb("bias_rep", [P, K, P])
        row0 = sb("row0", [P, 1])
        masked_u = sb("masked_u", [1, K * D])
        ident = sb("ident", [P, P])
        ones = sb("ones", [P, P])
        tiny = sb("tiny", [P, 1])
        seq = sb("seq", [P, CHUNKS, SEQ], I32)
        raw, eff, is_masked, is_last, keys = (outst[:, 0, i * SEQ:(i + 1) * SEQ] for i in range(5))
        top = sb("top", [P, 1 + SLOTS])
        counts = sb("counts", [P, 2])
        slot_index = sb("slot_index", [P, HALVES, SLOTS])
        slot_weight = sb("slot_weight", [P, HALVES, SLOTS])
        overflow = sb("overflow", [P, CHUNKS])
        overflow_any = sb("overflow_any", [P, 1])
        flag = sb("flag", [1, 1], I32)
        index = sb("index", [P, CHUNKS, TILES], I32)
        weight = sb("weight", [P, CHUNKS, TILES, HALVES])
        weight_k = sb("weight_k", [P, CHUNKS, PAIRS])
        masked_k = sb("masked_k", [1, CHUNKS, PAIRS])
        newest_index = sb("newest_index", [P, CHUNKS], I32)
        newest = sb("newest", [P, D])
        newestT = sb("newestT", [P, P])
        sums = sb("sums", [P, COLS])
        squares = sb("squares", [P, COLS])
        bias_row = squares[0:1, :]
        coef = sb("coef", [P, COLS])
        caps = sb("caps", [P, COLS])
        caps_sum = sb("caps_sum", [P, COLS])
        proj = sb("proj", [P, COLS])
        length = squares
        expd = squares
        factor = sb("factor", [P, COLS])
        shifted = factor
        peak = sb("peak", [P, PAIRS])
        total = sb("total", [P, PAIRS])
        ratio = sb("ratio", [P, PAIRS])
        final = [sb(f"final{i}", [P, P]) for i in range(2)]

        trans = [bank("trans0"), bank("trans1")]
        score = [bank("score0"), bank("score1")]
        acc = bank("acc")
        caps_ps = bank("caps_ps")
        norm = bank("norm")
        lists = bank("lists")

        seq_in = sem("seq_in")
        params_in = sem("params_in")
        table_in = [sem(f"table_in{i}") for i in range(STAGES)]
        gathered = [sem(f"gathered{i}") for i in range(2 * BLOCKS)]
        newest_in = sem("newest_in")
        ident_ready = sem("ident_ready")
        zeroed = sem("zeroed")
        bias_rep_ready = sem("bias_rep_ready")
        ones_ready = sem("ones_ready")
        wT_ps_ready = sem("wT_ps_ready")
        bias_ps_ready = sem("bias_ps_ready")
        masked_ps_ready = sem("masked_ps_ready")
        setup_out = sem("setup_out")
        slots_ready = sem("slots_ready")
        slotsT_ready = sem("slotsT_ready")
        index_ready = sem("index_ready")
        newest_index_ready = sem("newest_index_ready")
        weight_ready = sem("weight_ready")
        trans_full = sem("trans_full")
        trans_read = sem("trans_read")
        newestT_ps_ready = sem("newestT_ps_ready")
        acc_ready = sem("acc_ready")
        sums_ready = sem("sums_ready")
        caps_ps_ready = sem("caps_ps_ready")
        squares_ready = sem("squares_ready")
        norm_ready = sem("norm_ready")
        ln_ready = sem("ln_ready")
        length_ready = sem("length_ready")
        caps_ready = sem("caps_ready")
        proj_ps_ready = sem("proj_ps_ready")
        proj_ready = sem("proj_ready")
        logits_ready = sem("logits_ready")
        shifted_ready = sem("shifted_ready")
        expd_ready = sem("expd_ready")
        coef_ready = sem("coef_ready")
        match_in_ready = sem("match_in_ready")
        match_ready = sem("match_ready")
        match_shifted = sem("match_shifted")
        match_expd = sem("match_expd")
        final_ready = sem("final_ready")
        score_ready = sem("score_ready")
        score_read = sem("score_read")
        stored = [sem("stored0"), sem("stored1")]
        overflow_ready = sem("overflow_ready")
        overflow_ps_ready = sem("overflow_ps_ready")
        flag_ready = sem("flag_ready")
        dve_done = sem("dve_done")

        HALF = 2
        REST = SEQ - P
        g_index = rowsT[:, 0:HALF * BATCH].bitcast(I32).rearrange("p (i n) -> p i n", i=HALF)
        g_named = rowsT[:, HALF * BATCH:2 * HALF * BATCH].rearrange("p (i n) -> p i n", i=HALF)
        g_final = rowsT[:, 2 * HALF * BATCH:(2 * HALF + 1) * BATCH]
        g_rows, g_rowsT = rows[0][:, 0:HALF * D], rows[0][:, HALF * D:2 * HALF * D]
        g_live = peak[:, 0:HALF]
        g_index_now = index[:, 0, 0:HALF]
        g_named_now = ratio[:, 64:64 + HALF]
        g_coef = coef[:, 0:HALF * K].rearrange("p (i k) -> p i k", k=K)
        g_exp = expd[:, 0:HALF * K].rearrange("p (i k) -> p i k", k=K)
        g_exponent = shifted[:, 0:HALF * K].rearrange("p (i k) -> p i k", k=K)
        g_logits = caps_ps[:, 8:8 + HALF * K].rearrange("p (i k) -> p i k", k=K)
        g_listed = sem("g_listed")
        g_listed_ps = sem("g_listed_ps")
        g_lists_read = sem("g_lists_read")
        g_picked = sem("g_picked")
        g_taken = sem("g_taken")
        g_gathered = sem("g_gathered")
        g_trans_ready = sem("g_trans_ready")
        g_rowsT_ready = sem("g_rowsT_ready")
        g_coef_ready = sem("g_coef_ready")
        g_acc_ready = sem("g_acc_ready")
        g_sums_ready = sem("g_sums_ready")
        g_caps_ps_ready = sem("g_caps_ps_ready")
        g_squares_ready = sem("g_squares_ready")
        g_norm_ready = sem("g_norm_ready")
        g_ln_ready = sem("g_ln_ready")
        g_length_ready = sem("g_length_ready")
        g_caps_ready = sem("g_caps_ready")
        g_proj_ps_ready = sem("g_proj_ps_ready")
        g_proj_ready = sem("g_proj_ready")
        g_logits_ready = sem("g_logits_ready")
        g_shifted_ready = sem("g_shifted_ready")
        g_expd_ready = sem("g_expd_ready")
        g_match_in_ready = sem("g_match_in_ready")
        g_match_ready = sem("g_match_ready")
        g_match_shifted = sem("g_match_shifted")
        g_match_expd = sem("g_match_expd")
        g_final_ready = sem("g_final_ready")
        g_score_ready = sem("g_score_ready")
        g_score_read = sem("g_score_read")
        g_stored = [sem("g_stored0"), sem("g_stored1")]
        g_setup_done = sem("g_setup_done")
        g_dve_done = sem("g_dve_done")
        G_STEPS = 31

        def wanted(engine):
            engine.wait_ge(flag_ready, 1)
            return engine.If(engine.value_load(flag[0:1, 0:1], min_val=0, max_val=1) != 0)

        def main_path_over(engine):
            for i in range(2):
                engine.wait_ge(stored[i], 16 * (CHUNKS * STORES // 2))

        def by_k(t, k):
            return t[:, :].rearrange("p (n k) -> p n k", k=K)[:, :, k]

        def tile_cols(t, n):
            return t[:, n * HALVES * K:(n + 1) * HALVES * K]

        def each_k(t):
            return t[:, :].rearrange("p (n k) -> p n k", k=K)

        def over_k(t):
            return t.unsqueeze(2).to_broadcast([P, PAIRS, K])

        block = ctx.enter_context(nc.Block())

        @block.sync
        def _(sp):
            sp.dma_start(seq[:, :, :], r_seq.rearrange("(c p) s -> p c s", p=P)).then_inc(seq_in, 16)
            sp.dma_start(w[:, :], s_w).then_inc(params_in, 16)
            sp.dma_start(bias_row, s_b.unsqueeze(0)).then_inc(params_in, 16)
            sp.dma_start(bias_col[:, :], s_b.rearrange("(k e) -> e k", k=K),
                         allow_slow_non_contiguous=True).then_inc(params_in, 16)
            sp.dma_start(row0[:, :], table[0:1, :].rearrange("o d -> d o"),
                         allow_slow_non_contiguous=True).then_inc(params_in, 16)
            for g in range(GROUPS):
                parts, s = group_parts(g), g % STAGES
                if g >= STAGES:
                    sp.wait_ge(trans_full, fill_at[("table", g - STAGES)] + 1)
                sp.dma_start(stage[0:parts, s * GROUP:(s + 1) * GROUP],
                             table[g * GROUP:g * GROUP + parts * FILL, :].rearrange("(p j) d -> p (j d)", j=FILL)
                             ).then_inc(table_in[s], 16)
            for m in range(CHUNKS * STORES):
                c, part = divmod(m, STORES)
                sp.wait_ge(score_read, (m + 1) * STORE)
                sp.dma_start(out[c * P:(c + 1) * P, part * STORE * UNIT:(part + 1) * STORE * UNIT],
                             outst[:, m % 2, :]).then_inc(stored[m % 2], 16)
            main_path_over(sp)

            with wanted(sp):
                for m in range(CHUNKS * STORES):
                    c, part = divmod(m, STORES)
                    sp.wait_ge(g_score_read, (m + 1) * STORE)
                    sp.dma_start(out[c * P:(c + 1) * P, part * STORE * UNIT:(part + 1) * STORE * UNIT],
                                 outst[:, m % 2, :]).then_inc(g_stored[m % 2], 16)
                for i in range(2):
                    sp.wait_ge(g_stored[i], 16 * (CHUNKS * STORES // 2))

        @block.gpsimd
        def _(pool):
            nc.gpsimd.memset(ident[:, :], 0.0).then_inc(zeroed, 1)
            nc.gpsimd.memset(weight[:, :, :, :], 0.0).then_inc(zeroed, 1)
            pool.wait_ge(zeroed, 1)
            nc.gpsimd.affine_select(out=ident[:, :], in_=ident[:, :], compare_op=ALU.not_equal, fill=1.0, base=0,
                                    pattern=[[-1, P]], channel_multiplier=1).then_inc(ident_ready, 1)
            pool.wait_ge(params_in, 64)
            nc.gpsimd.tensor_copy(bias_rep[:, :, :], bias_col[:, :].unsqueeze(2).to_broadcast([P, K, P])
                                  ).then_inc(bias_rep_ready, 1)
            for c in range(CHUNKS):
                pool.wait_ge(index_ready, c + 1)
                if c == 1:
                    pool.wait_ge(trans_full, last_table_fill + 1)
                if c >= 2:
                    pool.wait_ge(acc_ready, STEPS * (c - 1))
                for t in range(TILES):
                    nc.gpsimd.indirect_dma_start(
                        out=rows[c % 2][:, t * D:(t + 1) * D], out_offset=None, in_=table,
                        in_offset=bass.IndirectOffsetOnAxis(ap=index[:, c, t:t + 1], axis=0)
                    ).then_inc(gathered[(c % 2) * BLOCKS + t // BLOCK], 16)
                pool.wait_ge(newest_index_ready, c + 1)
                if c >= 1:
                    pool.wait_ge(newestT_ps_ready, c)
                nc.gpsimd.indirect_dma_start(
                    out=newest[:, :], out_offset=None, in_=table,
                    in_offset=bass.IndirectOffsetOnAxis(ap=newest_index[:, c:c + 1], axis=0)
                ).then_inc(newest_in, 16)

            with wanted(pool):
                main_path_over(pool)
                with pool.Fori(0, BATCH) as n:
                    pool.wait_ge(g_picked, n + 1)
                    pool.sem_inc(g_taken, 1)
                    for i in range(HALF):
                        nc.gpsimd.indirect_dma_start(
                            out=g_rows[:, i * D:(i + 1) * D], out_offset=None, in_=table,
                            in_offset=bass.IndirectOffsetOnAxis(ap=g_index_now[:, i:i + 1], axis=0)
                        ).then_inc(g_gathered, 16)

        @block.scalar
        def _(act):
            def fill_out(n):
                act.wait_ge(trans_full, n + 1)
                f = fills[n]
                src = trans[n % 2]
                if f[0] == "table":
                    m = FILL * group_parts(f[1])
                    nc.scalar.copy(tableT[:, f[1] * GROUP:f[1] * GROUP + m].rearrange("d (p j) -> d j p", j=FILL),
                                   src[:, 0:m].rearrange("d (j p) -> d j p", j=FILL)).then_inc(trans_read, 1)
                else:
                    nc.scalar.copy(rowsT[:, f[2] * FILL * P:(f[2] + 1) * FILL * P], src[:, :]).then_inc(trans_read, 1)

            def score_out(c, j):
                u = c * UNITS + j
                m = u // STORE
                act.wait_ge(score_ready, u + 1)
                if j % STORE == 0 and m >= 2:
                    act.wait_ge(stored[m % 2], 16 * (m // 2))
                nc.scalar.copy(outst[:, m % 2, (j % STORE) * UNIT:(j % STORE + 1) * UNIT],
                               score[u % 2][:, 0:UNIT]).then_inc(score_read, 1)

            def exp_match(c):
                act.wait_ge(match_shifted, c + 1)
                nc.scalar.activation(expd[:, :], shifted[:, :], ACT.Exp).then_inc(match_expd, 1)

            act.wait_ge(wT_ps_ready, 1)
            nc.scalar.copy(wT[:, :], score[0][:, :]).then_inc(setup_out, 1)
            act.wait_ge(bias_ps_ready, 1)
            nc.scalar.copy(bias_all[:, :], score[1][:, :]).then_inc(setup_out, 1)
            act.wait_ge(masked_ps_ready, 1)
            nc.scalar.copy(masked_u[:, :], norm[0:1, :]).then_inc(setup_out, 1)
            n = 0
            for c in range(CHUNKS):
                until = fill_at[("items", c, TILES // FILL - 1)] if c else last_table_fill
                first = n
                while n <= max(until, fill_at[("items", c, TILES // FILL - 1)]):
                    fill_out(n)
                    n += 1
                    if c >= 1 and n == first + 2:
                        exp_match(c - 1)
                gap = iter(range(UNITS))
                for i in range(STEPS):
                    v = c * STEPS + i
                    act.wait_ge(acc_ready, v + 1)
                    m = PAIRS if i == 0 else COLS
                    nc.scalar.copy(sums[:, 0:m], acc[:, 0:m]).then_inc(sums_ready, 1)
                    act.wait_ge(caps_ps_ready, v + 1)
                    if c >= 1 and i == 0:
                        act.wait_ge(final_ready, c)
                    nc.scalar.activation(squares[:, :], caps_ps[:, :], ACT.Square).then_inc(squares_ready, 1)
                    act.wait_ge(norm_ready, v + 1)
                    nc.scalar.activation(length[:, :], norm[:, :], ACT.Ln, bias=tiny[:, 0:1]).then_inc(ln_ready, 1)
                    act.wait_ge(ln_ready, v + 1)
                    nc.scalar.activation(length[:, :], length[:, :], ACT.Exp, scale=0.5).then_inc(length_ready, 1)
                    if c >= 1:
                        for _ in range(GAPS[2 * i]):
                            score_out(c - 1, next(gap))
                    if i < STEPS - 1:
                        v = c * (STEPS - 1) + i
                        act.wait_ge(proj_ps_ready, v + 1)
                        nc.scalar.copy(proj[:, :], acc[:, :]).then_inc(proj_ready, 1)
                        for x in range(GAPS[2 * i + 1]):
                            if x == 1:
                                act.wait_ge(shifted_ready, v + 1)
                                nc.scalar.activation(expd[:, :], shifted[:, :], ACT.Exp).then_inc(expd_ready, 1)
                            if c >= 1:
                                score_out(c - 1, next(gap))
            exp_match(CHUNKS - 1)
            for j in range(UNITS):
                score_out(CHUNKS - 1, j)

            with wanted(act):
                main_path_over(act)
                with act.Fori(0, BATCH) as n:
                    act.wait_ge(g_trans_ready, n + 1)
                    nc.scalar.copy(g_rowsT, trans[0][:, 0:HALF * P]).then_inc(g_rowsT_ready, 1)
                    for i in range(STEPS):
                        act.wait_ge(g_acc_ready, n * STEPS + (i + 1))
                        nc.scalar.copy(sums[:, 0:K], acc[:, 0:K]).then_inc(g_sums_ready, 1)
                        act.wait_ge(g_caps_ps_ready, n * STEPS + (i + 1))
                        nc.scalar.activation(squares[:, 0:K], caps_ps[:, 0:K], ACT.Square).then_inc(g_squares_ready, 1)
                        act.wait_ge(g_norm_ready, n * STEPS + (i + 1))
                        nc.scalar.activation(length[:, 0:K], norm[:, 0:K], ACT.Ln, bias=tiny[:, 0:1]
                                             ).then_inc(g_ln_ready, 1)
                        act.wait_ge(g_ln_ready, n * STEPS + (i + 1))
                        nc.scalar.activation(length[:, 0:K], length[:, 0:K], ACT.Exp, scale=0.5
                                             ).then_inc(g_length_ready, 1)
                        if i < STEPS - 1:
                            act.wait_ge(g_proj_ps_ready, n * (STEPS - 1) + (i + 1))
                            nc.scalar.copy(proj[:, 0:K], acc[:, 8:8 + K]).then_inc(g_proj_ready, 1)
                            act.wait_ge(g_shifted_ready, n * (STEPS - 1) + (i + 1))
                            nc.scalar.activation(g_exp, g_exponent, ACT.Exp).then_inc(g_expd_ready, 1)
                    act.wait_ge(g_match_shifted, n + 1)
                    nc.scalar.activation(expd[:, 0:K], shifted[:, 0:K], ACT.Exp).then_inc(g_match_expd, 1)
                for u in range(CHUNKS * UNITS):
                    m = u // STORE
                    act.wait_ge(g_score_ready, u + 1)
                    if u % STORE == 0 and m >= 2:
                        act.wait_ge(g_stored[m % 2], 16 * (m // 2))
                    nc.scalar.copy(outst[:, m % 2, (u % STORE) * UNIT:(u % STORE + 1) * UNIT],
                                   score[u % 2][:, 0:UNIT]).then_inc(g_score_read, 1)

        @block.vector
        def _(dve):
            steps = [0]

            def then(ins):
                steps[0] += 1
                ins.then_inc(dve_done, 1)
                dve.wait_ge(dve_done, steps[0])

            def prepare(c):
                then(nc.vector.tensor_copy(raw, seq[:, c, :]))
                nc.vector.tensor_single_scalar(is_masked, raw, 0.0, ALU.is_equal)
                then(nc.vector.tensor_scalar(keys, raw, 0.0, float(ITEMS), ALU.is_lt, ALU.mult))
                then(nc.vector.tensor_tensor(eff, raw, keys, ALU.add))
                then(nc.vector.tensor_scalar(eff, eff, 0.0, float(ITEMS - 1), ALU.max, ALU.min))
                then(nc.vector.tensor_single_scalar(is_last, eff, float(ITEMS - 1), ALU.is_equal))
                nc.vector.tensor_copy(newest_index[:, c:c + 1], eff[:, SEQ - 1:SEQ]).then_inc(newest_index_ready, 1)
                nc.vector.reduce_sum(counts[:, 0:1], is_masked, axis=AX)
                then(nc.vector.reduce_sum(counts[:, 1:2], is_last, axis=AX))
                then(nc.vector.tensor_tensor(is_last, is_last, is_masked, ALU.add))
                then(nc.vector.scalar_tensor_tensor(keys, is_last, GONE, eff, ALU.mult, ALU.add))
                for r in range(SLOTS // 8):
                    eight = top[:, 1 + 8 * r:9 + 8 * r]
                    then(nc.vector.max(out=eight, in_=keys))
                    then(nc.vector.match_replace(out=keys, in_to_replace=eight, in_values=keys,
                                                 imm_value=GONE))
                nc.vector.tensor_single_scalar(overflow[:, c:c + 1], top[:, SLOTS:SLOTS + 1], 0.0, ALU.is_ge)
                for h in range(HALVES):
                    nc.vector.memset(slot_index[:, h, 0:1], float(ITEMS - 1))
                    nc.vector.tensor_scalar_max(slot_index[:, h, 1:SLOTS], top[:, 1:SLOTS], 0.0)
                    nc.vector.tensor_copy(slot_weight[:, h, 0:1], counts[:, 1:2])
                    last = nc.vector.tensor_single_scalar(slot_weight[:, h, 1:SLOTS], top[:, 1:SLOTS], 0.0, ALU.is_ge)
                last.then_inc(slots_ready, 1)
                dve.wait_ge(slotsT_ready, c + 1)
                if c == 0:
                    dve.wait_ge(zeroed, 2)
                for h in range(HALVES):
                    here = slice(h * SLOTS, (h + 1) * SLOTS)
                    last = nc.vector.tensor_copy(index[here, c, :], lists[here, h * TILES:(h + 1) * TILES])
                last.then_inc(index_ready, 1)
                for h in range(HALVES):
                    here = slice(h * SLOTS, (h + 1) * SLOTS)
                    last = nc.vector.tensor_copy(weight[here, c, :, h],
                                                 lists[here, P + h * TILES:P + (h + 1) * TILES])
                then(last)
                nc.vector.tensor_scalar_mul(weight_k[:, c, :], weight[:, c, :, :].rearrange("p t h -> p (t h)"), 1.0 / K)
                nc.vector.tensor_scalar_mul(masked_k[0:1, c, :].rearrange("p (t h) -> p h t", h=HALVES),
                                            lists[0:1, 2 * P:3 * P].rearrange("p (h t) -> p h t", h=HALVES),
                                            1.0 / K).then_inc(weight_ready, 1)

            def squash(dst, v):
                dve.wait_ge(ln_ready, v + 1)
                then(nc.vector.tensor_scalar_add(factor[:, :], norm[:, :], 1.0))
                dve.wait_ge(length_ready, v + 1)
                then(nc.vector.scalar_tensor_tensor(factor[:, :], length[:, :], EPS, factor[:, :], ALU.add, ALU.mult))
                then(nc.vector.reciprocal(factor[:, :], factor[:, :]))
                then(nc.vector.tensor_tensor(factor[:, :], norm[:, :], factor[:, :], ALU.mult))
                return nc.vector.tensor_tensor(dst[:, :], caps_ps[:, :], factor[:, :], ALU.mult)

            def shift(src):
                then(nc.vector.reduce_max(peak[:, :], each_k(src), axis=AX))
                return nc.vector.tensor_tensor(each_k(shifted), each_k(src), over_k(peak[:, :]), ALU.subtract)

            nc.vector.memset(tiny[:, :], TINY)
            nc.vector.memset(ones[:, :], 1.0).then_inc(ones_ready, 1)
            dve.wait_ge(seq_in, 16)
            for c in range(CHUNKS):
                prepare(c)
            nc.vector.reduce_max(overflow_any[:, :], overflow[:, :], axis=AX).then_inc(overflow_ready, 1)

            for c in range(CHUNKS):
                for i in range(STEPS):
                    v = c * STEPS + i
                    dve.wait_ge(norm_ready, v + 1)
                    if i == 0:
                        squash(caps_sum, v).then_inc(caps_ready, 1)
                    elif i < STEPS - 1:
                        then(squash(caps, v))
                        nc.vector.tensor_tensor(caps_sum[:, :], caps_sum[:, :], caps[:, :], ALU.add
                                                ).then_inc(caps_ready, 1)
                    else:
                        then(squash(caps, v))
                    if i < STEPS - 1:
                        dve.wait_ge(logits_ready, c * (STEPS - 1) + i + 1)
                        shift(caps_ps).then_inc(shifted_ready, 1)
                        dve.wait_ge(expd_ready, c * (STEPS - 1) + i + 1)
                        then(nc.vector.reduce_sum(total[:, :], each_k(expd), axis=AX))
                        then(nc.vector.reciprocal(ratio[:, :], total[:, :]))
                        then(nc.vector.tensor_tensor(ratio[:, :], ratio[:, :],
                                                     weight[:, c, :, :].rearrange("p t h -> p (t h)"), ALU.mult))
                        nc.vector.tensor_tensor(each_k(coef), each_k(expd), over_k(ratio[:, :]), ALU.mult
                                                ).then_inc(coef_ready, 1)
                dve.wait_ge(newestT_ps_ready, c + 1)
                if c == 0:
                    dve.wait_ge(overflow_ps_ready, 1)
                then(nc.vector.tensor_copy(newestT[:, :].rearrange("d (t h) -> d h t", h=HALVES),
                                           lists[:, 3 * P:4 * P].rearrange("d (h t) -> d h t", h=HALVES)))
                if c == 0:
                    nc.vector.tensor_scalar_min(flag[:, :], lists[0:1, 0:1], 1.0).then_inc(flag_ready, 1)
                nc.vector.tensor_tensor(each_k(factor), each_k(caps), over_k(newestT[:, :]), ALU.mult
                                        ).then_inc(match_in_ready, 1)
                dve.wait_ge(match_ready, c + 1)
                shift(norm).then_inc(match_shifted, 1)
                dve.wait_ge(match_expd, c + 1)
                nc.vector.reduce_sum(total[:, :], each_k(expd), axis=AX)
                then(nc.vector.tensor_tensor(factor[:, :], expd[:, :], caps[:, :], ALU.mult))
                nc.vector.reciprocal(ratio[:, :], total[:, :])
                then(nc.vector.reduce_sum(peak[:, :], each_k(factor), axis=AX))
                if c >= 2:
                    dve.wait_ge(score_ready, (c - 1) * UNITS)
                nc.vector.tensor_tensor(final[c % 2][:, :].rearrange("e (h t) -> e h t", h=HALVES),
                                        peak[:, :].rearrange("e (t h) -> e h t", h=HALVES),
                                        ratio[:, :].rearrange("e (t h) -> e h t", h=HALVES), ALU.mult
                                        ).then_inc(final_ready, 1)

            with wanted(dve):
                main_path_over(dve)
                setup = [0]

                def settle(ins):
                    setup[0] += 1
                    ins.then_inc(g_setup_done, 1)
                    dve.wait_ge(g_setup_done, setup[0])

                nc.vector.memset(g_live, 0.0)
                nc.vector.memset(g_index, 0)
                settle(nc.vector.memset(g_named, 1.0))
                nc.vector.memset(g_live[:, 0:1], 1.0)
                settle(nc.vector.memset(g_live[0:REST, 1:2], 1.0))
                for c in range(CHUNKS):
                    settle(nc.vector.tensor_copy(raw, seq[:, c, :]))
                    nc.vector.tensor_single_scalar(is_masked, raw, 0.0, ALU.not_equal)
                    settle(nc.vector.tensor_scalar(keys, raw, 0.0, float(ITEMS), ALU.is_lt, ALU.mult))
                    settle(nc.vector.tensor_tensor(eff, raw, keys, ALU.add))
                    nc.vector.tensor_scalar(eff, eff, 0.0, float(ITEMS - 1), ALU.max, ALU.min).then_inc(g_listed, 1)
                    dve.wait_ge(g_listed_ps, c + 1)
                    for i, count in enumerate((P, REST)):
                        nc.vector.tensor_copy(g_index[0:count, i, c * P:(c + 1) * P],
                                              lists[0:count, i * P:(i + 1) * P])
                        last = nc.vector.tensor_copy(g_named[0:count, i, c * P:(c + 1) * P],
                                                     lists[0:count, (2 + i) * P:(3 + i) * P])
                    last.then_inc(g_lists_read, 1)
                    dve.wait_ge(g_lists_read, c + 1)

                with dve.Fori(0, BATCH) as n:
                    done = [0]

                    def then_(ins):
                        done[0] += 1
                        ins.then_inc(g_dve_done, 1)
                        dve.wait_ge(g_dve_done, n * G_STEPS + done[0])

                    def over_tiles(t):
                        return t.unsqueeze(2).to_broadcast([P, HALF, K])

                    nc.vector.tensor_copy(g_index_now, g_index[:, :, bass.ds(n, 1)].rearrange("p i o -> p (i o)")
                                          ).then_inc(g_picked, 1)
                    then_(nc.vector.tensor_copy(g_named_now,
                                                g_named[:, :, bass.ds(n, 1)].rearrange("p i o -> p (i o)")))
                    nc.vector.tensor_scalar_mul(g_coef, over_tiles(g_live), 1.0 / K).then_inc(g_coef_ready, 1)
                    for i in range(STEPS):
                        dve.wait_ge(g_ln_ready, n * STEPS + (i + 1))
                        then_(nc.vector.tensor_scalar_add(factor[:, 0:K], norm[:, 0:K], 1.0))
                        dve.wait_ge(g_length_ready, n * STEPS + (i + 1))
                        then_(nc.vector.scalar_tensor_tensor(factor[:, 0:K], length[:, 0:K], EPS, factor[:, 0:K],
                                                             ALU.add, ALU.mult))
                        then_(nc.vector.reciprocal(factor[:, 0:K], factor[:, 0:K]))
                        then_(nc.vector.tensor_tensor(factor[:, 0:K], norm[:, 0:K], factor[:, 0:K], ALU.mult))
                        if i == 0:
                            nc.vector.tensor_tensor(caps_sum[:, 0:K], caps_ps[:, 0:K], factor[:, 0:K], ALU.mult
                                                    ).then_inc(g_caps_ready, 1)
                        else:
                            then_(nc.vector.tensor_tensor(caps[:, 0:K], caps_ps[:, 0:K], factor[:, 0:K], ALU.mult))
                        if i == STEPS - 1:
                            break
                        if i > 0:
                            nc.vector.tensor_tensor(caps_sum[:, 0:K], caps_sum[:, 0:K], caps[:, 0:K], ALU.add
                                                    ).then_inc(g_caps_ready, 1)
                        dve.wait_ge(g_logits_ready, n * (STEPS - 1) + (i + 1))
                        then_(nc.vector.tensor_tensor(g_exponent, g_logits, over_tiles(g_named_now), ALU.mult))
                        then_(nc.vector.reduce_max(total[:, 0:HALF], g_exponent, axis=AX))
                        nc.vector.tensor_tensor(g_exponent, g_exponent, over_tiles(total[:, 0:HALF]), ALU.subtract
                                                ).then_inc(g_shifted_ready, 1)
                        dve.wait_ge(g_expd_ready, n * (STEPS - 1) + (i + 1))
                        then_(nc.vector.reduce_sum(total[:, 0:HALF], g_exp, axis=AX))
                        then_(nc.vector.reciprocal(ratio[:, 0:HALF], total[:, 0:HALF]))
                        then_(nc.vector.tensor_tensor(ratio[:, 0:HALF], ratio[:, 0:HALF], g_live, ALU.mult))
                        nc.vector.tensor_tensor(g_coef, g_exp, over_tiles(ratio[:, 0:HALF]), ALU.mult
                                                ).then_inc(g_coef_ready, 1)
                    newest_row = g_rowsT[:, SEQ - 1:SEQ]
                    nc.vector.tensor_scalar(factor[:, 0:K], caps[:, 0:K], newest_row, None, ALU.mult
                                            ).then_inc(g_match_in_ready, 1)
                    dve.wait_ge(g_match_ready, n + 1)
                    then_(nc.vector.reduce_max(total[:, 0:1], norm[:, 0:K], axis=AX))
                    nc.vector.tensor_scalar(shifted[:, 0:K], norm[:, 0:K], total[:, 0:1], None, ALU.subtract
                                            ).then_inc(g_match_shifted, 1)
                    dve.wait_ge(g_match_expd, n + 1)
                    then_(nc.vector.reduce_sum(total[:, 0:1], expd[:, 0:K], axis=AX))
                    then_(nc.vector.tensor_tensor(factor[:, 0:K], expd[:, 0:K], caps[:, 0:K], ALU.mult))
                    then_(nc.vector.reciprocal(ratio[:, 0:1], total[:, 0:1]))
                    then_(nc.vector.reduce_sum(total[:, 1:2], factor[:, 0:K], axis=AX))
                    then_(nc.vector.tensor_tensor(g_final[:, bass.ds(n, 1)], total[:, 1:2], ratio[:, 0:1], ALU.mult))
                    assert done[0] == G_STEPS, done[0]
                nc.vector.tensor_copy(total[:, 0:1], total[:, 0:1]).then_inc(g_final_ready, 1)

        @block.tensor
        def _(pe):
            def fill(n):
                f = fills[n]
                if n >= 2:
                    pe.wait_ge(trans_read, n - 1)
                if f[0] == "table":
                    g, parts = f[1], group_parts(f[1])
                    pe.wait_ge(table_in[g % STAGES], 16 * (g // STAGES + 1))
                    for j in range(FILL):
                        at = (g % STAGES) * GROUP + j * D
                        last = nc.tensor.transpose(trans[n % 2][:, j * parts:(j + 1) * parts],
                                                   stage[0:parts, at:at + D], ident[0:parts, 0:parts])
                else:
                    for j in range(FILL):
                        t = f[2] * FILL + j
                        last = nc.tensor.transpose(trans[n % 2][:, j * P:(j + 1) * P],
                                                   rows[f[1] % 2][:, t * D:(t + 1) * D], ident[:, :])
                last.then_inc(trans_full, 1)

            def slots_back(c):
                pe.wait_ge(slots_ready, c + 1)
                if c >= 1:
                    pe.wait_ge(weight_ready, c)
                nc.tensor.transpose(lists[:, 0:P], slot_index[:, :, :].rearrange("p h s -> p (h s)"), ident[:, :])
                nc.tensor.transpose(lists[:, P:2 * P], slot_weight[:, :, :].rearrange("p h s -> p (h s)"), ident[:, :])
                nc.tensor.matmul(lists[0:1, 2 * P:3 * P], counts[:, 0:1], ident[:, :], start=True, stop=True
                                 ).then_inc(slotsT_ready, 1)

            def score_unit(c, j):
                u = c * UNITS + j
                if j == 0:
                    pe.wait_ge(final_ready, c + 1)
                if u == 0:
                    pe.wait_ge(trans_read, last_table_fill + 1)
                if u >= 2:
                    pe.wait_ge(score_read, u - 1)
                nc.tensor.matmul(score[u % 2][:, 0:UNIT], final[c % 2][:, :], tableT[:, j * UNIT:(j + 1) * UNIT],
                                 start=True, stop=True).then_inc(score_ready, 1)

            def tile(t, c):
                return rows[c % 2][:, t * D:(t + 1) * D]

            pe.wait_ge(ident_ready, 1)
            pe.wait_ge(params_in, 64)
            pe.wait_ge(ones_ready, 1)
            for k in range(K):
                last = nc.tensor.transpose(score[0][:, k * P:(k + 1) * P], w[:, k * D:(k + 1) * D], ident[:, :])
            last.then_inc(wT_ps_ready, 1)
            nc.tensor.matmul(score[1][:, :], ones[0:1, :], bias_row, start=True, stop=True
                             ).then_inc(bias_ps_ready, 1)
            nc.tensor.matmul(norm[0:1, :], row0[:, 0:1], w[:, :], start=True, stop=False)
            nc.tensor.matmul(norm[0:1, :], ones[0:1, 0:1], bias_row, start=False, stop=True
                             ).then_inc(masked_ps_ready, 1)
            slots_back(0)
            n = 0
            for _ in table_fills(-1):
                fill(n)
                n += 1
            for c in range(CHUNKS):
                pe.wait_ge(weight_ready, c + 1)
                for blk in range(BLOCKS):
                    pe.wait_ge(gathered[(c % 2) * BLOCKS + blk], 16 * BLOCK * (c // 2 + 1))
                    for t in range(blk * BLOCK, (blk + 1) * BLOCK):
                        last = nc.tensor.matmul(acc[:, t * HALVES:(t + 1) * HALVES], tile(t, c),
                                                weight_k[:, c, t * HALVES:(t + 1) * HALVES], start=True, stop=True)
                    if blk == BLOCKS - 1:
                        last.then_inc(acc_ready, 1)
                    for _ in range(BLOCK // FILL):
                        fill(n)
                        n += 1
                    if c == 0:
                        if blk < CHUNKS - 1:
                            slots_back(blk + 1)
                        for _ in table_fills(blk):
                            fill(n)
                            n += 1
                pe.wait_ge(newest_in, 16 * (c + 1))
                if c == 0:
                    pe.wait_ge(weight_ready, CHUNKS)
                nc.tensor.transpose(lists[:, 3 * P:4 * P], newest[:, :], ident[:, :]).then_inc(newestT_ps_ready, 1)
                if c == 0:
                    pe.wait_ge(overflow_ready, 1)
                    nc.tensor.matmul(lists[0:1, 0:1], ones[:, 0:1], overflow_any[:, 0:1], start=True, stop=True
                                     ).then_inc(overflow_ps_ready, 1)
                gap = iter(range(UNITS))
                for i in range(STEPS):
                    v = c * STEPS + i
                    if i > 0:
                        pe.wait_ge(coef_ready, c * (STEPS - 1) + i)
                        for t in range(TILES):
                            last = nc.tensor.matmul(tile_cols(acc, t), tile(t, c), tile_cols(coef, t),
                                                    start=True, stop=True)
                        last.then_inc(acc_ready, 1)
                    pe.wait_ge(sums_ready, v + 1)
                    if c == 0 and i == 0:
                        pe.wait_ge(setup_out, 3)
                    for k in range(K):
                        dst, wk = by_k(caps_ps, k), slice(k * D, (k + 1) * D)
                        nc.tensor.matmul(dst, w[:, wk], sums[:, 0:PAIRS] if i == 0 else by_k(sums, k),
                                         start=True, stop=False)
                        nc.tensor.matmul(dst, bias_all[:, wk], weight_k[:, c, :] if i == 0 else by_k(coef, k),
                                         start=False, stop=False)
                        last = nc.tensor.matmul(dst, masked_u[0:1, wk], masked_k[0:1, c, :], start=False, stop=True)
                    last.then_inc(caps_ps_ready, 1)
                    pe.wait_ge(squares_ready, v + 1)
                    if c >= 1 and i == 0:
                        pe.wait_ge(match_shifted, c)
                    nc.tensor.matmul(norm[:, :], ones[:, :], squares[:, :], start=True, stop=True
                                     ).then_inc(norm_ready, 1)
                    if c >= 1:
                        for _ in range(GAPS[2 * i]):
                            score_unit(c - 1, next(gap))
                    if i < STEPS - 1:
                        pe.wait_ge(caps_ready, c * (STEPS - 1) + i + 1)
                        for k in range(K):
                            last = nc.tensor.matmul(by_k(acc, k), wT[:, k * D:(k + 1) * D], by_k(caps_sum, k),
                                                    start=True, stop=True)
                        last.then_inc(proj_ps_ready, 1)
                        if c == 0 and i == 0:
                            pe.wait_ge(bias_rep_ready, 1)
                        for k in range(K):
                            nc.tensor.matmul(by_k(caps_ps, k), bias_rep[:, k, :], by_k(caps_sum, k),
                                             start=(k == 0), stop=False, skip_group_check=True)
                        pe.wait_ge(proj_ready, c * (STEPS - 1) + i + 1)
                        if i == 0:
                            pe.wait_ge(trans_read, fill_at[("items", c, TILES // FILL - 1)] + 1)
                        for t in range(TILES):
                            last = nc.tensor.matmul(tile_cols(caps_ps, t), rowsT[:, t * P:(t + 1) * P],
                                                    tile_cols(proj, t), start=False, stop=(t == TILES - 1),
                                                    skip_group_check=True)
                        last.then_inc(logits_ready, 1)
                        if c >= 1:
                            for _ in range(GAPS[2 * i + 1]):
                                score_unit(c - 1, next(gap))
                pe.wait_ge(match_in_ready, c + 1)
                nc.tensor.matmul(norm[:, :], ones[:, :], factor[:, :], start=True, stop=True
                                 ).then_inc(match_ready, 1)
            for j in range(UNITS):
                score_unit(CHUNKS - 1, j)

            with wanted(pe):
                main_path_over(pe)
                for c in range(CHUNKS):
                    pe.wait_ge(g_listed, c + 1)
                    if c >= 1:
                        pe.wait_ge(g_lists_read, c)
                    for i, part in enumerate((slice(0, P), slice(P, SEQ))):
                        count = part.stop - part.start
                        nc.tensor.transpose(lists[0:count, i * P:(i + 1) * P], eff[:, part], ident[:, :])
                        last = nc.tensor.transpose(lists[0:count, (2 + i) * P:(3 + i) * P], is_masked[:, part],
                                                   ident[:, :])
                    last.then_inc(g_listed_ps, 1)

                with pe.Fori(0, BATCH) as n:
                    pe.wait_ge(g_gathered, n * (16 * HALF) + 16 * HALF)
                    for i in range(HALF):
                        last = nc.tensor.transpose(trans[0][:, i * P:(i + 1) * P], g_rows[:, i * D:(i + 1) * D],
                                                   ident[:, :])
                    last.then_inc(g_trans_ready, 1)
                    for i in range(STEPS):
                        pe.wait_ge(g_coef_ready, n * STEPS + (i + 1))
                        for t in range(HALF):
                            last = nc.tensor.matmul(acc[:, 0:K], g_rows[:, t * D:(t + 1) * D], g_coef[:, t, :],
                                                    start=(t == 0), stop=(t == HALF - 1))
                        last.then_inc(g_acc_ready, 1)
                        pe.wait_ge(g_sums_ready, n * STEPS + (i + 1))
                        for k in range(K):
                            nc.tensor.matmul(caps_ps[:, k:k + 1], w[:, k * D:(k + 1) * D], sums[:, k:k + 1],
                                             start=True, stop=False)
                            for t in range(HALF):
                                last = nc.tensor.matmul(caps_ps[:, k:k + 1], bias_all[:, k * D:(k + 1) * D],
                                                        g_coef[:, t, k:k + 1], start=False, stop=(t == HALF - 1))
                        last.then_inc(g_caps_ps_ready, 1)
                        pe.wait_ge(g_squares_ready, n * STEPS + (i + 1))
                        nc.tensor.matmul(norm[:, 0:K], ones[:, :], squares[:, 0:K], start=True, stop=True
                                         ).then_inc(g_norm_ready, 1)
                        if i == STEPS - 1:
                            break
                        pe.wait_ge(g_caps_ready, n * (STEPS - 1) + (i + 1))
                        for k in range(K):
                            last = nc.tensor.matmul(acc[:, 8 + k:9 + k], wT[:, k * D:(k + 1) * D],
                                                    caps_sum[:, k:k + 1], start=True, stop=True)
                        last.then_inc(g_proj_ps_ready, 1)
                        pe.wait_ge(g_proj_ready, n * (STEPS - 1) + (i + 1))
                        if i == 0:
                            pe.wait_ge(g_rowsT_ready, n + 1)
                        for t in range(HALF):
                            for k in range(K):
                                nc.tensor.matmul(g_logits[:, t, k:k + 1], bias_rep[:, k, :], caps_sum[:, k:k + 1],
                                                 start=(t == 0 and k == 0), stop=False, skip_group_check=True)
                            last = nc.tensor.matmul(g_logits[:, t, :], g_rowsT[:, t * P:(t + 1) * P], proj[:, 0:K],
                                                    start=False, stop=(t == HALF - 1), skip_group_check=True)
                        last.then_inc(g_logits_ready, 1)
                    pe.wait_ge(g_match_in_ready, n + 1)
                    nc.tensor.matmul(norm[:, 0:K], ones[:, :], factor[:, 0:K], start=True, stop=True
                                     ).then_inc(g_match_ready, 1)

                pe.wait_ge(g_final_ready, 1)
                for u in range(CHUNKS * UNITS):
                    c, j = divmod(u, UNITS)
                    if u >= 2:
                        pe.wait_ge(g_score_read, u - 1)
                    nc.tensor.matmul(score[u % 2][:, 0:UNIT], g_final[:, c * P:(c + 1) * P],
                                     tableT[:, j * UNIT:(j + 1) * UNIT], start=True, stop=True
                                     ).then_inc(g_score_ready, 1)


_INS = ["r_seq", "L0_rec_emb_table", "L0_rec_s_w", "L0_rec_s_b"]


def kernel(**inputs):
    import numpy as np
    import concourse.bacc as bacc
    from concourse.bass_utils import run_bass_kernel_spmd

    nc = bacc.Bacc("TRN2", target_bir_lowering=False, num_devices=1)
    arrays, args = {}, []
    for name in _INS:
        a = np.ascontiguousarray(inputs[name])
        arrays[f"in_{name}"] = a
        args.append(nc.dram_tensor(f"in_{name}", a.shape, mybir.dt.from_np(a.dtype), kind="ExternalInput").ap())
    shape = (inputs["r_seq"].shape[0], inputs["L0_rec_emb_table"].shape[0])
    args.append(nc.dram_tensor("scores", shape, F32, kind="ExternalOutput").ap())
    capsule_routing(nc, *args)
    result = run_bass_kernel_spmd(nc, [arrays], core_ids=[0])
    return result.results[0]["scores"]
```

```python
from contextlib import ExitStack

import concourse.bass as bass
from concourse import mybir

F32 = mybir.dt.float32
F16 = mybir.dt.float16
BF16 = mybir.dt.bfloat16
I32 = mybir.dt.int32
ALU = mybir.AluOpType
ACT = mybir.ActivationFunctionType
AX = mybir.AxisListType.X

P = 128
STEPS = 3


def capsule_routing(nc, r_seq, table, s_w, s_b, out):
    BATCH, SEQ = r_seq.shape
    ITEMS, D = table.shape
    K = s_w.shape[1] // D
    assert D == P and BATCH % P == 0 and s_b.shape[0] == K * D
    CHUNKS = BATCH // P
    SLOTS = 64
    HALVES = P // SLOTS
    TILES = P // HALVES
    PAIRS = TILES * HALVES
    COLS = PAIRS * K
    BLOCK = 8
    BLOCKS = TILES // BLOCK
    FILL = 4
    GONE = -30000.0
    EPS = 1e-12
    TINY = 1e-30

    GROUP = FILL * P
    GROUPS = -(-ITEMS // GROUP)
    STAGES = 8
    UNIT = 500
    UNITS = ITEMS // UNIT
    assert UNITS * UNIT == ITEMS
    STORE = 1
    STORES = UNITS // STORE
    SLOTS_OUT = 5
    PARTS = 2
    PEAKS = 5
    GAPS = [7, 4, 6, 4, 4]
    assert sum(GAPS) == UNITS and STORES * STORE == UNITS

    def group_parts(g):
        return min(GROUP, ITEMS - g * GROUP) // FILL

    assert all(group_parts(g) * FILL == min(GROUP, ITEMS - g * GROUP) for g in range(GROUPS))

    fills = [("table", g) for g in range(GROUPS)]
    fills += [("items", c, q) for c in range(CHUNKS) for q in range(TILES // FILL)]
    fill_at = {f: n for n, f in enumerate(fills)}
    reader = ["act" if f[0] == "table" or f[2] % 2 == 0 else "dve" for f in fills]

    def reads(engine, n):
        return reader[:n + 1].count(engine)

    ctx = ExitStack()
    with ctx:
        def sb(name, shape, dt=F32):
            return ctx.enter_context(nc.sbuf_tensor(name, shape, dt))

        def bank(name, banks=1):
            return ctx.enter_context(nc.psum_tensor(name, [P, banks * 512], F32))

        def sem(name):
            return ctx.enter_context(nc.semaphore(name))

        tableT = sb("tableT", [P, ITEMS])
        rows = sb("rows", [P, TILES * D])
        split = sb("split", [P, TILES, PARTS, D], F16)
        splitT = sb("splitT", [P, TILES, PARTS, P], F16)
        outst = sb("outst", [P, SLOTS_OUT, STORE * UNIT])
        stage = split[:, :, :, :].rearrange("p t i d -> p (t i d)").bitcast(F32)
        w = sb("w", [P, K * D])
        wT = sb("wT", [P, K * D])
        bias_col = sb("bias_col", [P, K])
        bias_all = sb("bias_all", [P, K * D])
        bias_rep = sb("bias_rep", [P, K, P])
        ident16 = sb("ident16", [P, P], F16)
        table_peak = sb("table_peak", [P, PEAKS + 1])
        scale_row = sb("scale_row", [1, 4], I32)
        scale = sb("scale", [P, 2])
        row0 = sb("row0", [P, 1])
        masked_u = sb("masked_u", [1, K * D])
        ident = sb("ident", [P, P])
        ones = sb("ones", [P, P])
        tiny = sb("tiny", [P, 1])
        seq = sb("seq", [P, CHUNKS, SEQ], I32)
        scratch = outst[:, :, :].rearrange("p m n -> p (m n)")
        raw, eff, is_masked, is_last, keys = (scratch[:, i * SEQ:(i + 1) * SEQ] for i in range(5))
        top = sb("top", [P, 1 + SLOTS])
        counts = sb("counts", [P, 2])
        slot_index = sb("slot_index", [P, HALVES, SLOTS])
        slot_weight = sb("slot_weight", [P, HALVES, SLOTS])
        overflow = sb("overflow", [P, CHUNKS])
        overflow_any = sb("overflow_any", [P, 1])
        flag = sb("flag", [1, 1], I32)
        index = sb("index", [P, CHUNKS, TILES], I32)
        weight = sb("weight", [P, CHUNKS, TILES, HALVES])
        weight_k = sb("weight_k", [P, CHUNKS, PAIRS])
        weight_kb = sb("weight_kb", [P, CHUNKS, PAIRS], BF16)
        masked_k = sb("masked_k", [1, CHUNKS, PAIRS])
        newest_index = sb("newest_index", [P, CHUNKS], I32)
        newest = sb("newest", [P, D])
        newestT = sb("newestT", [P, P])
        sums = sb("sums", [P, COLS])
        squares = sb("squares", [P, COLS])
        bias_row = squares[0:1, :]
        coef_parts = sb("coef_parts", [P, 2, COLS])
        coef = coef_parts[:, 0, :]
        coef_low = sb("coef_low", [P, COLS], BF16)
        caps = sb("caps", [P, COLS])
        caps_sum = sb("caps_sum", [P, COLS])
        proj_parts = sb("proj_parts", [P, 2, COLS])
        proj = proj_parts[:, 0, :]
        proj_low = sb("proj_low", [P, COLS], BF16)
        length = squares
        expd = squares
        factor = sb("factor", [P, COLS])
        shifted = factor
        peak = sb("peak", [P, PAIRS])
        total = sb("total", [P, PAIRS])
        ratio = sb("ratio", [P, PAIRS])
        final = [sb(f"final{i}", [P, P]) for i in range(2)]

        trans = [bank("trans0"), bank("trans1")]
        score = [bank("score0"), bank("score1")]
        acc = bank("acc", 2)
        caps_ps = bank("caps_ps")
        norm = bank("norm")
        lists = norm

        seq_in = sem("seq_in")
        params_in = sem("params_in")
        table_in = [sem(f"table_in{i}") for i in range(STAGES)]
        gathered = [sem(f"gathered{i}") for i in range(BLOCKS)]
        ident16_ready = sem("ident16_ready")
        table_peak_ready = sem("table_peak_ready")
        table_peak_ps_ready = sem("table_peak_ps_ready")
        scale_row_ready = sem("scale_row_ready")
        scale_ps_ready = sem("scale_ps_ready")
        scale_ready = sem("scale_ready")
        w_scaled = sem("w_scaled")
        high_ready = sem("high_ready")
        low_ready = sem("low_ready")
        newestT_ready = sem("newestT_ready")
        proj_copied = sem("proj_copied")
        newest_in = sem("newest_in")
        ident_ready = sem("ident_ready")
        zeroed = sem("zeroed")
        bias_rep_ready = sem("bias_rep_ready")
        ones_ready = sem("ones_ready")
        wT_ps_ready = sem("wT_ps_ready")
        bias_ps_ready = sem("bias_ps_ready")
        masked_ps_ready = sem("masked_ps_ready")
        setup_out = sem("setup_out")
        slots_ready = sem("slots_ready")
        slotsT_ready = sem("slotsT_ready")
        index_ready = sem("index_ready")
        newest_index_ready = sem("newest_index_ready")
        weight_ready = sem("weight_ready")
        trans_full = sem("trans_full")
        trans_read = {"act": sem("trans_read_act"), "dve": sem("trans_read_dve")}
        newestT_ps_ready = sem("newestT_ps_ready")
        acc_ready = sem("acc_ready")
        sums_ready = sem("sums_ready")
        caps_ps_ready = sem("caps_ps_ready")
        squares_ready = sem("squares_ready")
        norm_ready = sem("norm_ready")
        ln_ready = sem("ln_ready")
        length_ready = sem("length_ready")
        caps_ready = sem("caps_ready")
        proj_ps_ready = sem("proj_ps_ready")
        proj_ready = sem("proj_ready")
        logits_ready = sem("logits_ready")
        shifted_ready = sem("shifted_ready")
        expd_ready = sem("expd_ready")
        coef_ready = sem("coef_ready")
        match_in_ready = sem("match_in_ready")
        match_ready = sem("match_ready")
        match_shifted = sem("match_shifted")
        match_expd = sem("match_expd")
        final_ready = sem("final_ready")
        score_ready = sem("score_ready")
        score_read = sem("score_read")
        stored = [sem(f"stored{i}") for i in range(SLOTS_OUT)]
        overflow_ready = sem("overflow_ready")
        overflow_ps_ready = sem("overflow_ps_ready")
        flag_ready = sem("flag_ready")
        dve_done = sem("dve_done")

        HALF = 2
        REST = SEQ - P
        words = splitT[:, :, :, :].rearrange("p t i d -> p (t i d)").bitcast(F32)
        g_index = words[:, 0:HALF * BATCH].bitcast(I32).rearrange("p (i n) -> p i n", i=HALF)
        g_named = words[:, HALF * BATCH:2 * HALF * BATCH].rearrange("p (i n) -> p i n", i=HALF)
        g_final = words[:, 2 * HALF * BATCH:(2 * HALF + 1) * BATCH]
        g_rows, g_rowsT = rows[:, 0:HALF * D], rows[:, HALF * D:2 * HALF * D]
        g_live = peak[:, 0:HALF]
        g_index_now = index[:, 0, 0:HALF]
        g_named_now = ratio[:, 64:64 + HALF]
        g_coef = coef[:, 0:HALF * K].rearrange("p (i k) -> p i k", k=K)
        g_exp = expd[:, 0:HALF * K].rearrange("p (i k) -> p i k", k=K)
        g_exponent = shifted[:, 0:HALF * K].rearrange("p (i k) -> p i k", k=K)
        g_logits = caps_ps[:, 8:8 + HALF * K].rearrange("p (i k) -> p i k", k=K)
        g_listed = sem("g_listed")
        g_listed_ps = sem("g_listed_ps")
        g_lists_read = sem("g_lists_read")
        g_picked = sem("g_picked")
        g_taken = sem("g_taken")
        g_gathered = sem("g_gathered")
        g_trans_ready = sem("g_trans_ready")
        g_rowsT_ready = sem("g_rowsT_ready")
        g_coef_ready = sem("g_coef_ready")
        g_acc_ready = sem("g_acc_ready")
        g_sums_ready = sem("g_sums_ready")
        g_caps_ps_ready = sem("g_caps_ps_ready")
        g_squares_ready = sem("g_squares_ready")
        g_norm_ready = sem("g_norm_ready")
        g_ln_ready = sem("g_ln_ready")
        g_length_ready = sem("g_length_ready")
        g_caps_ready = sem("g_caps_ready")
        g_proj_ps_ready = sem("g_proj_ps_ready")
        g_proj_ready = sem("g_proj_ready")
        g_logits_ready = sem("g_logits_ready")
        g_shifted_ready = sem("g_shifted_ready")
        g_expd_ready = sem("g_expd_ready")
        g_match_in_ready = sem("g_match_in_ready")
        g_match_ready = sem("g_match_ready")
        g_match_shifted = sem("g_match_shifted")
        g_match_expd = sem("g_match_expd")
        g_final_ready = sem("g_final_ready")
        g_score_ready = sem("g_score_ready")
        g_score_read = sem("g_score_read")
        g_stored = [sem(f"g_stored{i}") for i in range(SLOTS_OUT)]
        g_setup_done = sem("g_setup_done")
        g_dve_done = sem("g_dve_done")
        G_STEPS = 31

        def wanted(engine):
            engine.wait_ge(flag_ready, 1)
            return engine.If(engine.value_load(flag[0:1, 0:1], min_val=0, max_val=1) != 0)

        def main_path_over(engine):
            for i in range(SLOTS_OUT):
                engine.wait_ge(stored[i], 16 * (CHUNKS * STORES // SLOTS_OUT))

        def by_k(t, k):
            return t.rearrange("p (n k) -> p n k", k=K)[:, :, k]

        def each_k(t):
            return t.rearrange("p (n k) -> p n k", k=K)

        def over_k(t):
            return t.unsqueeze(2).to_broadcast([P, PAIRS, K])

        def top_half(t):
            return t.bitcast(BF16).rearrange("... (n two) -> ... n two", two=2)[..., 1]

        HK = HALVES * K
        acc_parts = acc[:, :].rearrange("p (t i c) -> p t i c", i=2, c=HK)
        acc_sides = acc[:, :].rearrange("p (t i c) -> p t c i", i=2, c=HK)

        def by_tile(t):
            return t.rearrange("p (t c) -> p t c", c=HK)

        rows_by_tile = rows[:, :].rearrange("p (t d) -> p t d", d=D)
        assert BLOCK // FILL == 2

        block = ctx.enter_context(nc.Block())

        @block.sync
        def _(sp):
            sp.dma_start(seq[:, :, :], r_seq.rearrange("(c p) s -> p c s", p=P)).then_inc(seq_in, 16)
            sp.dma_start(w[:, :], s_w).then_inc(params_in, 16)
            sp.dma_start(bias_row, s_b.unsqueeze(0)).then_inc(params_in, 16)
            sp.dma_start(bias_col[:, :], s_b.rearrange("(k e) -> e k", k=K),
                         allow_slow_non_contiguous=True).then_inc(params_in, 16)
            sp.dma_start(row0[:, :], table[0:1, :].rearrange("o d -> d o"),
                         allow_slow_non_contiguous=True).then_inc(params_in, 16)
            for g in range(GROUPS):
                parts, s = group_parts(g), g % STAGES
                if g >= STAGES:
                    sp.wait_ge(trans_full, fill_at[("table", g - STAGES)] + 1)
                sp.dma_start(stage[0:parts, s * GROUP:(s + 1) * GROUP],
                             table[g * GROUP:g * GROUP + parts * FILL, :].rearrange("(p j) d -> p (j d)", j=FILL)
                             ).then_inc(table_in[s], 16)
            for m in range(CHUNKS * STORES):
                c, part = divmod(m, STORES)
                sp.wait_ge(score_read, (m + 1) * STORE)
                sp.dma_start(out[c * P:(c + 1) * P, part * STORE * UNIT:(part + 1) * STORE * UNIT],
                             outst[:, m % SLOTS_OUT, :]).then_inc(stored[m % SLOTS_OUT], 16)
            main_path_over(sp)

            with wanted(sp):
                for m in range(CHUNKS * STORES):
                    c, part = divmod(m, STORES)
                    sp.wait_ge(g_score_read, (m + 1) * STORE)
                    sp.dma_start(out[c * P:(c + 1) * P, part * STORE * UNIT:(part + 1) * STORE * UNIT],
                                 outst[:, m % SLOTS_OUT, :]).then_inc(g_stored[m % SLOTS_OUT], 16)
                for i in range(SLOTS_OUT):
                    sp.wait_ge(g_stored[i], 16 * (CHUNKS * STORES // SLOTS_OUT))

        @block.gpsimd
        def _(pool):
            nc.gpsimd.memset(ident[:, :], 0.0).then_inc(zeroed, 1)
            nc.gpsimd.memset(weight[:, :, :, :], 0.0).then_inc(zeroed, 1)
            pool.wait_ge(zeroed, 1)
            nc.gpsimd.affine_select(out=ident[:, :], in_=ident[:, :], compare_op=ALU.not_equal, fill=1.0, base=0,
                                    pattern=[[-1, P]], channel_multiplier=1).then_inc(ident_ready, 1)
            pool.wait_ge(ident_ready, 1)
            nc.gpsimd.tensor_copy(ident16[:, :], ident[:, :]).then_inc(ident16_ready, 1)
            pool.wait_ge(params_in, 64)
            nc.gpsimd.tensor_copy(bias_rep[:, :, :], bias_col[:, :].unsqueeze(2).to_broadcast([P, K, P])
                                  ).then_inc(bias_rep_ready, 1)
            for c in range(CHUNKS):
                pool.wait_ge(index_ready, c + 1)
                for t in range(TILES):
                    if c >= 1 and t % BLOCK == 0:
                        pool.wait_ge(high_ready, (c - 1) * BLOCKS + t // BLOCK + 1)
                        pool.wait_ge(low_ready, (c - 1) * BLOCKS + t // BLOCK + 1)
                    nc.gpsimd.indirect_dma_start(
                        out=rows[:, t * D:(t + 1) * D], out_offset=None, in_=table,
                        in_offset=bass.IndirectOffsetOnAxis(ap=index[:, c, t:t + 1], axis=0)
                    ).then_inc(gathered[t // BLOCK], 16)
                pool.wait_ge(newest_index_ready, c + 1)
                if c >= 1:
                    pool.wait_ge(newestT_ps_ready, c)
                nc.gpsimd.indirect_dma_start(
                    out=newest[:, :], out_offset=None, in_=table,
                    in_offset=bass.IndirectOffsetOnAxis(ap=newest_index[:, c:c + 1], axis=0)
                ).then_inc(newest_in, 16)

            with wanted(pool):
                main_path_over(pool)
                with pool.Fori(0, BATCH) as n:
                    pool.wait_ge(g_picked, n + 1)
                    pool.sem_inc(g_taken, 1)
                    for i in range(HALF):
                        nc.gpsimd.indirect_dma_start(
                            out=g_rows[:, i * D:(i + 1) * D], out_offset=None, in_=table,
                            in_offset=bass.IndirectOffsetOnAxis(ap=g_index_now[:, i:i + 1], axis=0)
                        ).then_inc(g_gathered, 16)

        @block.scalar
        def _(act):
            def fill_out(n):
                act.wait_ge(trans_full, n + 1)
                f = fills[n]
                src = trans[n % 2]
                if f[0] == "table":
                    m = FILL * group_parts(f[1])
                    nc.scalar.copy(tableT[:, f[1] * GROUP:f[1] * GROUP + m].rearrange("d (p j) -> d j p", j=FILL),
                                   src[:, 0:m].rearrange("d (j p) -> d j p", j=FILL)).then_inc(trans_read["act"], 1)
                else:
                    nc.scalar.copy(splitT[:, f[2] * FILL:(f[2] + 1) * FILL, :, :].rearrange("p t i s -> p (t i s)"),
                                   src[:, :].bitcast(F16)).then_inc(trans_read["act"], 1)

            def score_out(c, j):
                u = c * UNITS + j
                m = u // STORE
                act.wait_ge(score_ready, u + 1)
                if j % STORE == 0 and m >= SLOTS_OUT:
                    act.wait_ge(stored[m % SLOTS_OUT], 16 * (m // SLOTS_OUT))
                nc.scalar.copy(outst[:, m % SLOTS_OUT, (j % STORE) * UNIT:(j % STORE + 1) * UNIT],
                               score[u % 2][:, 0:UNIT]).then_inc(score_read, 1)

            def exp_match(c):
                act.wait_ge(match_shifted, c + 1)
                nc.scalar.activation(expd[:, :], shifted[:, :], ACT.Exp).then_inc(match_expd, 1)

            act.wait_ge(wT_ps_ready, 1)
            nc.scalar.copy(wT[:, :], score[0][:, :]).then_inc(setup_out, 1)
            act.wait_ge(bias_ps_ready, 1)
            nc.scalar.copy(bias_all[:, :], score[1][:, :]).then_inc(setup_out, 1)
            act.wait_ge(masked_ps_ready, 1)
            nc.scalar.copy(masked_u[:, :], norm[0:1, :]).then_inc(setup_out, 1)
            for g in range(GROUPS):
                fill_out(g)
            act.wait_ge(scale_ready, 1)
            for c in range(CHUNKS):
                for blk in range(BLOCKS):
                    act.wait_ge(gathered[blk], 16 * BLOCK * (c + 1))
                    if c >= 1 and blk == 0:
                        act.wait_ge(acc_ready, STEPS * c)
                    here = slice(blk * BLOCK, (blk + 1) * BLOCK)
                    nc.scalar.activation(split[:, here, 0, :], rows_by_tile[:, here, :], ACT.Copy, scale=scale[:, 0:1]
                                         ).then_inc(high_ready, 1)
                    if c >= 1 and blk == 1:
                        exp_match(c - 1)
                    if blk >= 1:
                        fill_out(fill_at[("items", c, (blk - 1) * BLOCK // FILL)])
                fill_out(fill_at[("items", c, (BLOCKS - 1) * BLOCK // FILL)])
                gap = iter(range(UNITS))
                for i in range(STEPS):
                    v = c * STEPS + i
                    if i == 0:
                        act.wait_ge(acc_ready, v + 1)
                        nc.scalar.copy(sums[:, 0:PAIRS], acc[:, 0:PAIRS]).then_inc(sums_ready, 1)
                    act.wait_ge(caps_ps_ready, v + 1)
                    if c >= 1 and i == 0:
                        act.wait_ge(final_ready, c)
                    nc.scalar.activation(squares[:, :], caps_ps[:, :], ACT.Square).then_inc(squares_ready, 1)
                    act.wait_ge(norm_ready, v + 1)
                    nc.scalar.activation(length[:, :], norm[:, :], ACT.Ln, bias=tiny[:, 0:1]).then_inc(ln_ready, 1)
                    act.wait_ge(ln_ready, v + 1)
                    nc.scalar.activation(length[:, :], length[:, :], ACT.Exp, scale=0.5).then_inc(length_ready, 1)
                    if c >= 1:
                        for _ in range(GAPS[2 * i]):
                            score_out(c - 1, next(gap))
                    if i < STEPS - 1:
                        v = c * (STEPS - 1) + i
                        act.wait_ge(proj_ps_ready, v + 1)
                        nc.scalar.copy(proj, acc[:, 0:COLS]).then_inc(proj_copied, 1)
                        for x in range(GAPS[2 * i + 1]):
                            if x == 1:
                                act.wait_ge(shifted_ready, v + 1)
                                nc.scalar.activation(expd[:, :], shifted[:, :], ACT.Exp).then_inc(expd_ready, 1)
                            if c >= 1:
                                score_out(c - 1, next(gap))
            exp_match(CHUNKS - 1)
            for j in range(UNITS):
                score_out(CHUNKS - 1, j)

            with wanted(act):
                main_path_over(act)
                with act.Fori(0, BATCH) as n:
                    act.wait_ge(g_trans_ready, n + 1)
                    nc.scalar.copy(g_rowsT, trans[0][:, 0:HALF * P]).then_inc(g_rowsT_ready, 1)
                    for i in range(STEPS):
                        act.wait_ge(g_acc_ready, n * STEPS + (i + 1))
                        nc.scalar.copy(sums[:, 0:K], acc[:, 0:K]).then_inc(g_sums_ready, 1)
                        act.wait_ge(g_caps_ps_ready, n * STEPS + (i + 1))
                        nc.scalar.activation(squares[:, 0:K], caps_ps[:, 0:K], ACT.Square).then_inc(g_squares_ready, 1)
                        act.wait_ge(g_norm_ready, n * STEPS + (i + 1))
                        nc.scalar.activation(length[:, 0:K], norm[:, 0:K], ACT.Ln, bias=tiny[:, 0:1]
                                             ).then_inc(g_ln_ready, 1)
                        act.wait_ge(g_ln_ready, n * STEPS + (i + 1))
                        nc.scalar.activation(length[:, 0:K], length[:, 0:K], ACT.Exp, scale=0.5
                                             ).then_inc(g_length_ready, 1)
                        if i < STEPS - 1:
                            act.wait_ge(g_proj_ps_ready, n * (STEPS - 1) + (i + 1))
                            nc.scalar.copy(proj[:, 0:K], acc[:, 8:8 + K]).then_inc(g_proj_ready, 1)
                            act.wait_ge(g_shifted_ready, n * (STEPS - 1) + (i + 1))
                            nc.scalar.activation(g_exp, g_exponent, ACT.Exp).then_inc(g_expd_ready, 1)
                    act.wait_ge(g_match_shifted, n + 1)
                    nc.scalar.activation(expd[:, 0:K], shifted[:, 0:K], ACT.Exp).then_inc(g_match_expd, 1)
                for u in range(CHUNKS * UNITS):
                    m = u // STORE
                    act.wait_ge(g_score_ready, u + 1)
                    if u % STORE == 0 and m >= SLOTS_OUT:
                        act.wait_ge(g_stored[m % SLOTS_OUT], 16 * (m // SLOTS_OUT))
                    nc.scalar.copy(outst[:, m % SLOTS_OUT, (u % STORE) * UNIT:(u % STORE + 1) * UNIT],
                                   score[u % 2][:, 0:UNIT]).then_inc(g_score_read, 1)

        @block.vector
        def _(dve):
            steps = [0]

            def then(ins):
                steps[0] += 1
                ins.then_inc(dve_done, 1)
                dve.wait_ge(dve_done, steps[0])

            def prepare(c):
                then(nc.vector.tensor_copy(raw, seq[:, c, :]))
                nc.vector.tensor_single_scalar(is_masked, raw, 0.0, ALU.is_equal)
                then(nc.vector.tensor_scalar(keys, raw, 0.0, float(ITEMS), ALU.is_lt, ALU.mult))
                then(nc.vector.tensor_tensor(eff, raw, keys, ALU.add))
                then(nc.vector.tensor_scalar(eff, eff, 0.0, float(ITEMS - 1), ALU.max, ALU.min))
                then(nc.vector.tensor_single_scalar(is_last, eff, float(ITEMS - 1), ALU.is_equal))
                nc.vector.tensor_copy(newest_index[:, c:c + 1], eff[:, SEQ - 1:SEQ]).then_inc(newest_index_ready, 1)
                nc.vector.reduce_sum(counts[:, 0:1], is_masked, axis=AX)
                then(nc.vector.reduce_sum(counts[:, 1:2], is_last, axis=AX))
                then(nc.vector.tensor_tensor(is_last, is_last, is_masked, ALU.add))
                then(nc.vector.scalar_tensor_tensor(keys, is_last, GONE, eff, ALU.mult, ALU.add))
                for r in range(SLOTS // 8):
                    eight = top[:, 1 + 8 * r:9 + 8 * r]
                    then(nc.vector.max(out=eight, in_=keys))
                    then(nc.vector.match_replace(out=keys, in_to_replace=eight, in_values=keys,
                                                 imm_value=GONE))
                nc.vector.tensor_single_scalar(overflow[:, c:c + 1], top[:, SLOTS:SLOTS + 1], 0.0, ALU.is_ge)
                for h in range(HALVES):
                    nc.vector.memset(slot_index[:, h, 0:1], float(ITEMS - 1))
                    nc.vector.tensor_scalar_max(slot_index[:, h, 1:SLOTS], top[:, 1:SLOTS], 0.0)
                    nc.vector.tensor_copy(slot_weight[:, h, 0:1], counts[:, 1:2])
                    last = nc.vector.tensor_single_scalar(slot_weight[:, h, 1:SLOTS], top[:, 1:SLOTS], 0.0, ALU.is_ge)
                last.then_inc(slots_ready, 1)
                dve.wait_ge(slotsT_ready, c + 1)
                if c == 0:
                    dve.wait_ge(zeroed, 2)
                for h in range(HALVES):
                    here = slice(h * SLOTS, (h + 1) * SLOTS)
                    last = nc.vector.tensor_copy(index[here, c, :], lists[here, h * TILES:(h + 1) * TILES])
                last.then_inc(index_ready, 1)
                for h in range(HALVES):
                    here = slice(h * SLOTS, (h + 1) * SLOTS)
                    last = nc.vector.tensor_copy(weight[here, c, :, h],
                                                 lists[here, P + h * TILES:P + (h + 1) * TILES])
                then(last)
                nc.vector.tensor_scalar_mul(weight_kb[:, c, :], weight[:, c, :, :].rearrange("p t h -> p (t h)"), 1.0 / K)
                nc.vector.tensor_scalar_mul(weight_k[:, c, :], weight[:, c, :, :].rearrange("p t h -> p (t h)"), 1.0 / K)
                nc.vector.tensor_scalar_mul(masked_k[0:1, c, :].rearrange("p (t h) -> p h t", h=HALVES),
                                            lists[0:1, 2 * P:3 * P].rearrange("p (h t) -> p h t", h=HALVES),
                                            1.0 / K).then_inc(weight_ready, 1)

            def squash(dst, v):
                dve.wait_ge(ln_ready, v + 1)
                then(nc.vector.tensor_scalar_add(factor[:, :], norm[:, :], 1.0))
                dve.wait_ge(length_ready, v + 1)
                then(nc.vector.scalar_tensor_tensor(factor[:, :], length[:, :], EPS, factor[:, :], ALU.add, ALU.mult))
                then(nc.vector.reciprocal(factor[:, :], factor[:, :]))
                then(nc.vector.tensor_tensor(factor[:, :], norm[:, :], factor[:, :], ALU.mult))
                return nc.vector.tensor_tensor(dst[:, :], caps_ps[:, :], factor[:, :], ALU.mult)

            def shift(src):
                then(nc.vector.reduce_max(peak[:, :], each_k(src), axis=AX))
                return nc.vector.tensor_tensor(each_k(shifted[:, :]), each_k(src), over_k(peak[:, :]), ALU.subtract)

            def cut(parts, low):
                then(nc.vector.tensor_tensor(parts[:, 1, :], parts[:, 0, :], top_half(parts[:, 0, :]), ALU.subtract))
                return nc.vector.tensor_tensor(low[:, :], parts[:, 1, :], top_half(parts[:, 1, :]), ALU.subtract)

            def table_peak_of(m):
                size = ITEMS // PEAKS
                last_group = min(GROUPS - 1, ((m + 1) * size - 1) // GROUP)
                dve.wait_ge(trans_read["act"], reads("act", fill_at[("table", last_group)]))
                return nc.vector.tensor_reduce(out=table_peak[:, m:m + 1], in_=tableT[:, m * size:(m + 1) * size],
                                               axis=AX, op=ALU.max, apply_absolute_value=True)

            nc.vector.memset(tiny[:, :], TINY)
            nc.vector.memset(ones[:, :], 1.0).then_inc(ones_ready, 1)
            dve.wait_ge(seq_in, 16)
            for c in range(CHUNKS):
                prepare(c)
                table_peak_of(c)
            then(table_peak_of(CHUNKS))
            nc.vector.reduce_max(table_peak[:, PEAKS:PEAKS + 1], table_peak[:, 0:PEAKS], axis=AX
                                 ).then_inc(table_peak_ready, 1)
            dve.wait_ge(table_peak_ps_ready, 1)
            then(nc.vector.reduce_max(scale_row[0:1, 2:3].bitcast(F32), caps_ps[0:1, 0:P], axis=AX))
            then(nc.vector.tensor_single_scalar(scale_row[0:1, 2:3], scale_row[0:1, 2:3], 23, ALU.logical_shift_right))
            then(nc.vector.tensor_scalar_max(scale_row[0:1, 3:4], scale_row[0:1, 2:3], 64.0))
            nc.vector.tensor_scalar(scale_row[0:1, 0:1], scale_row[0:1, 3:4], -1.0, 268.0, ALU.mult, ALU.add)
            then(nc.vector.tensor_scalar_add(scale_row[0:1, 1:2], scale_row[0:1, 3:4], -14.0))
            nc.vector.tensor_single_scalar(scale_row[0:1, 0:2], scale_row[0:1, 0:2], 23, ALU.logical_shift_left
                                           ).then_inc(scale_row_ready, 1)
            dve.wait_ge(scale_ps_ready, 1)
            then(nc.vector.tensor_copy(scale[:, :], caps_ps[:, P:P + 2]))
            dve.wait_ge(setup_out, 3)
            nc.vector.tensor_scalar(w[:, :], w[:, :], scale[:, 1:2], None, ALU.mult).then_inc(scale_ready, 1)
            nc.vector.tensor_scalar(wT[:, :], wT[:, :], scale[:, 1:2], None, ALU.mult).then_inc(w_scaled, 1)
            nc.vector.reduce_max(overflow_any[:, :], overflow[:, :], axis=AX).then_inc(overflow_ready, 1)

            def attend(c):
                dve.wait_ge(match_ready, c + 1)
                shift(norm[:, :]).then_inc(match_shifted, 1)
                dve.wait_ge(match_expd, c + 1)
                nc.vector.reduce_sum(total[:, :], each_k(expd[:, :]), axis=AX)
                then(nc.vector.tensor_tensor(factor[:, :], expd[:, :], caps[:, :], ALU.mult))
                nc.vector.reciprocal(ratio[:, :], total[:, :])
                then(nc.vector.reduce_sum(peak[:, :], each_k(factor[:, :]), axis=AX))
                if c >= 2:
                    dve.wait_ge(score_ready, (c - 1) * UNITS)
                nc.vector.tensor_tensor(final[c % 2][:, :].rearrange("e (h t) -> e h t", h=HALVES),
                                        peak[:, :].rearrange("e (t h) -> e h t", h=HALVES),
                                        ratio[:, :].rearrange("e (t h) -> e h t", h=HALVES), ALU.mult
                                        ).then_inc(final_ready, 1)

            def fill_out(n):
                q = fills[n][2]
                dve.wait_ge(trans_full, n + 1)
                nc.vector.tensor_copy(splitT[:, q * FILL:(q + 1) * FILL, :, :].rearrange("p t i s -> p (t i s)"),
                                      trans[n % 2][:, :].bitcast(F16)).then_inc(trans_read["dve"], 1)

            for c in range(CHUNKS):
                for blk in range(BLOCKS):
                    dve.wait_ge(high_ready, c * BLOCKS + blk + 1)
                    here = slice(blk * BLOCK, (blk + 1) * BLOCK)
                    nc.vector.scalar_tensor_tensor(split[:, here, 1, :], rows_by_tile[:, here, :], scale[:, 0:1],
                                                   split[:, here, 0, :], ALU.mult, ALU.subtract
                                                   ).then_inc(low_ready, 1)
                    if c >= 1 and blk == 0:
                        attend(c - 1)
                    if blk >= 1:
                        fill_out(fill_at[("items", c, (blk - 1) * BLOCK // FILL + 1)])
                fill_out(fill_at[("items", c, (BLOCKS - 1) * BLOCK // FILL + 1)])
                dve.wait_ge(newestT_ps_ready, c + 1)
                nc.vector.tensor_copy(newestT[:, :].rearrange("d (t h) -> d h t", h=HALVES),
                                      lists[:, 0:P].rearrange("d (h t) -> d h t", h=HALVES)).then_inc(newestT_ready, 1)
                if c == 0:
                    dve.wait_ge(overflow_ps_ready, 1)
                    nc.vector.tensor_scalar_min(flag[:, :], lists[0:1, P:P + 1], 1.0).then_inc(flag_ready, 1)
                for i in range(STEPS):
                    v = c * STEPS + i
                    if i > 0:
                        dve.wait_ge(acc_ready, v + 1)
                        nc.vector.reduce_sum(by_tile(sums[:, :]), acc_sides, axis=AX).then_inc(sums_ready, 1)
                    dve.wait_ge(norm_ready, v + 1)
                    if i == 0:
                        squash(caps_sum, v).then_inc(caps_ready, 1)
                    elif i < STEPS - 1:
                        then(squash(caps, v))
                        nc.vector.tensor_tensor(caps_sum[:, :], caps_sum[:, :], caps[:, :], ALU.add
                                                ).then_inc(caps_ready, 1)
                    else:
                        then(squash(caps, v))
                    if i < STEPS - 1:
                        x = c * (STEPS - 1) + i + 1
                        dve.wait_ge(proj_copied, x)
                        cut(proj_parts, proj_low).then_inc(proj_ready, 1)
                        dve.wait_ge(logits_ready, x)
                        then(nc.vector.reduce_sum(by_tile(shifted[:, :]), acc_sides, axis=AX))
                        then(nc.vector.tensor_tensor(shifted[:, :], shifted[:, :], caps_ps[:, :], ALU.add))
                        shift(shifted[:, :]).then_inc(shifted_ready, 1)
                        dve.wait_ge(expd_ready, x)
                        then(nc.vector.reduce_sum(total[:, :], each_k(expd[:, :]), axis=AX))
                        then(nc.vector.reciprocal(ratio[:, :], total[:, :]))
                        then(nc.vector.tensor_tensor(ratio[:, :], ratio[:, :],
                                                     weight[:, c, :, :].rearrange("p t h -> p (t h)"), ALU.mult))
                        then(nc.vector.tensor_tensor(each_k(coef), each_k(expd[:, :]), over_k(ratio[:, :]), ALU.mult))
                        cut(coef_parts, coef_low).then_inc(coef_ready, 1)
                nc.vector.tensor_tensor(each_k(factor[:, :]), each_k(caps[:, :]), over_k(newestT[:, :]), ALU.mult
                                        ).then_inc(match_in_ready, 1)
            attend(CHUNKS - 1)

            with wanted(dve):
                main_path_over(dve)
                setup = [0]

                def settle(ins):
                    setup[0] += 1
                    ins.then_inc(g_setup_done, 1)
                    dve.wait_ge(g_setup_done, setup[0])

                nc.vector.memset(g_live, 0.0)
                nc.vector.memset(g_index, 0)
                nc.vector.tensor_scalar(w[:, :], w[:, :], scale[:, 0:1], None, ALU.mult)
                nc.vector.tensor_scalar(wT[:, :], wT[:, :], scale[:, 0:1], None, ALU.mult)
                settle(nc.vector.memset(g_named, 1.0))
                nc.vector.memset(g_live[:, 0:1], 1.0)
                settle(nc.vector.memset(g_live[0:REST, 1:2], 1.0))
                for c in range(CHUNKS):
                    settle(nc.vector.tensor_copy(raw, seq[:, c, :]))
                    nc.vector.tensor_single_scalar(is_masked, raw, 0.0, ALU.not_equal)
                    settle(nc.vector.tensor_scalar(keys, raw, 0.0, float(ITEMS), ALU.is_lt, ALU.mult))
                    settle(nc.vector.tensor_tensor(eff, raw, keys, ALU.add))
                    nc.vector.tensor_scalar(eff, eff, 0.0, float(ITEMS - 1), ALU.max, ALU.min).then_inc(g_listed, 1)
                    dve.wait_ge(g_listed_ps, c + 1)
                    for i, count in enumerate((P, REST)):
                        nc.vector.tensor_copy(g_index[0:count, i, c * P:(c + 1) * P],
                                              lists[0:count, i * P:(i + 1) * P])
                        last = nc.vector.tensor_copy(g_named[0:count, i, c * P:(c + 1) * P],
                                                     lists[0:count, (2 + i) * P:(3 + i) * P])
                    last.then_inc(g_lists_read, 1)
                    dve.wait_ge(g_lists_read, c + 1)

                with dve.Fori(0, BATCH) as n:
                    done = [0]

                    def then_(ins):
                        done[0] += 1
                        ins.then_inc(g_dve_done, 1)
                        dve.wait_ge(g_dve_done, n * G_STEPS + done[0])

                    def over_tiles(t):
                        return t.unsqueeze(2).to_broadcast([P, HALF, K])

                    nc.vector.tensor_copy(g_index_now, g_index[:, :, bass.ds(n, 1)].rearrange("p i o -> p (i o)")
                                          ).then_inc(g_picked, 1)
                    then_(nc.vector.tensor_copy(g_named_now,
                                                g_named[:, :, bass.ds(n, 1)].rearrange("p i o -> p (i o)")))
                    nc.vector.tensor_scalar_mul(g_coef, over_tiles(g_live), 1.0 / K).then_inc(g_coef_ready, 1)
                    for i in range(STEPS):
                        dve.wait_ge(g_ln_ready, n * STEPS + (i + 1))
                        then_(nc.vector.tensor_scalar_add(factor[:, 0:K], norm[:, 0:K], 1.0))
                        dve.wait_ge(g_length_ready, n * STEPS + (i + 1))
                        then_(nc.vector.scalar_tensor_tensor(factor[:, 0:K], length[:, 0:K], EPS, factor[:, 0:K],
                                                             ALU.add, ALU.mult))
                        then_(nc.vector.reciprocal(factor[:, 0:K], factor[:, 0:K]))
                        then_(nc.vector.tensor_tensor(factor[:, 0:K], norm[:, 0:K], factor[:, 0:K], ALU.mult))
                        if i == 0:
                            nc.vector.tensor_tensor(caps_sum[:, 0:K], caps_ps[:, 0:K], factor[:, 0:K], ALU.mult
                                                    ).then_inc(g_caps_ready, 1)
                        else:
                            then_(nc.vector.tensor_tensor(caps[:, 0:K], caps_ps[:, 0:K], factor[:, 0:K], ALU.mult))
                        if i == STEPS - 1:
                            break
                        if i > 0:
                            nc.vector.tensor_tensor(caps_sum[:, 0:K], caps_sum[:, 0:K], caps[:, 0:K], ALU.add
                                                    ).then_inc(g_caps_ready, 1)
                        dve.wait_ge(g_logits_ready, n * (STEPS - 1) + (i + 1))
                        then_(nc.vector.tensor_tensor(g_exponent, g_logits, over_tiles(g_named_now), ALU.mult))
                        then_(nc.vector.reduce_max(total[:, 0:HALF], g_exponent, axis=AX))
                        nc.vector.tensor_tensor(g_exponent, g_exponent, over_tiles(total[:, 0:HALF]), ALU.subtract
                                                ).then_inc(g_shifted_ready, 1)
                        dve.wait_ge(g_expd_ready, n * (STEPS - 1) + (i + 1))
                        then_(nc.vector.reduce_sum(total[:, 0:HALF], g_exp, axis=AX))
                        then_(nc.vector.reciprocal(ratio[:, 0:HALF], total[:, 0:HALF]))
                        then_(nc.vector.tensor_tensor(ratio[:, 0:HALF], ratio[:, 0:HALF], g_live, ALU.mult))
                        nc.vector.tensor_tensor(g_coef, g_exp, over_tiles(ratio[:, 0:HALF]), ALU.mult
                                                ).then_inc(g_coef_ready, 1)
                    newest_row = g_rowsT[:, SEQ - 1:SEQ]
                    nc.vector.tensor_scalar(factor[:, 0:K], caps[:, 0:K], newest_row, None, ALU.mult
                                            ).then_inc(g_match_in_ready, 1)
                    dve.wait_ge(g_match_ready, n + 1)
                    then_(nc.vector.reduce_max(total[:, 0:1], norm[:, 0:K], axis=AX))
                    nc.vector.tensor_scalar(shifted[:, 0:K], norm[:, 0:K], total[:, 0:1], None, ALU.subtract
                                            ).then_inc(g_match_shifted, 1)
                    dve.wait_ge(g_match_expd, n + 1)
                    then_(nc.vector.reduce_sum(total[:, 0:1], expd[:, 0:K], axis=AX))
                    then_(nc.vector.tensor_tensor(factor[:, 0:K], expd[:, 0:K], caps[:, 0:K], ALU.mult))
                    then_(nc.vector.reciprocal(ratio[:, 0:1], total[:, 0:1]))
                    then_(nc.vector.reduce_sum(total[:, 1:2], factor[:, 0:K], axis=AX))
                    then_(nc.vector.tensor_tensor(g_final[:, bass.ds(n, 1)], total[:, 1:2], ratio[:, 0:1], ALU.mult))
                    assert done[0] == G_STEPS, done[0]
                nc.vector.tensor_copy(total[:, 0:1], total[:, 0:1]).then_inc(g_final_ready, 1)

        @block.tensor
        def _(pe):
            def fill(n):
                f = fills[n]
                if n >= 2:
                    pe.wait_ge(trans_read[reader[n - 2]], reads(reader[n - 2], n - 2))
                if f[0] == "table":
                    g, parts = f[1], group_parts(f[1])
                    pe.wait_ge(table_in[g % STAGES], 16 * (g // STAGES + 1))
                    for j in range(FILL):
                        at = (g % STAGES) * GROUP + j * D
                        last = nc.tensor.transpose(trans[n % 2][:, j * parts:(j + 1) * parts],
                                                   stage[0:parts, at:at + D], ident[0:parts, 0:parts])
                else:
                    dst = trans[n % 2][:, :].bitcast(F16)
                    for j in range(FILL * PARTS):
                        last = nc.tensor.transpose(dst[:, j * P:(j + 1) * P],
                                                   split[:, f[2] * FILL + j // PARTS, j % PARTS, :], ident16[:, :])
                last.then_inc(trans_full, 1)

            def slots_back(c):
                pe.wait_ge(slots_ready, c + 1)
                if c >= 1:
                    pe.wait_ge(weight_ready, c)
                nc.tensor.transpose(lists[:, 0:P], slot_index[:, :, :].rearrange("p h s -> p (h s)"), ident[:, :])
                nc.tensor.transpose(lists[:, P:2 * P], slot_weight[:, :, :].rearrange("p h s -> p (h s)"), ident[:, :])
                nc.tensor.matmul(lists[0:1, 2 * P:3 * P], counts[:, 0:1], ident[:, :], start=True, stop=True
                                 ).then_inc(slotsT_ready, 1)

            def score_unit(c, j):
                u = c * UNITS + j
                if j == 0:
                    pe.wait_ge(final_ready, c + 1)
                if u == 0:
                    pe.wait_ge(trans_read["act"], GROUPS)
                if u >= 2:
                    pe.wait_ge(score_read, u - 1)
                nc.tensor.matmul(score[u % 2][:, 0:UNIT], final[c % 2][:, :], tableT[:, j * UNIT:(j + 1) * UNIT],
                                 start=True, stop=True).then_inc(score_ready, 1)

            def tile_products(lhs, parts, low):
                for t in range(TILES):
                    here = slice(t * HK, (t + 1) * HK)
                    two = top_half(parts[:, :, here])
                    nc.tensor.matmul(acc_parts[:, t, :, :], lhs[:, t, 0, :], two, start=True, stop=False)
                    nc.tensor.matmul(acc_parts[:, t, :, :], lhs[:, t, 1, :], two, start=False, stop=False)
                    last = nc.tensor.matmul(acc_parts[:, t, 1, :], lhs[:, t, 0, :], low[:, here],
                                            start=False, stop=True)
                return last

            pe.wait_ge(ident_ready, 1)
            pe.wait_ge(params_in, 64)
            pe.wait_ge(ones_ready, 1)
            for k in range(K):
                last = nc.tensor.transpose(score[0][:, k * P:(k + 1) * P], w[:, k * D:(k + 1) * D], ident[:, :])
            last.then_inc(wT_ps_ready, 1)
            nc.tensor.matmul(score[1][:, :], ones[0:1, :], bias_row, start=True, stop=True
                             ).then_inc(bias_ps_ready, 1)
            nc.tensor.matmul(norm[0:1, :], row0[:, 0:1], w[:, :], start=True, stop=False)
            nc.tensor.matmul(norm[0:1, :], ones[0:1, 0:1], bias_row, start=False, stop=True
                             ).then_inc(masked_ps_ready, 1)
            pe.wait_ge(setup_out, 3)
            slots_back(0)
            for g in range(GROUPS):
                fill(g)
                if g % 7 == 5 and g // 7 < CHUNKS - 1:
                    slots_back(g // 7 + 1)
            pe.wait_ge(table_peak_ready, 1)
            nc.tensor.matmul(caps_ps[0:1, 0:P], table_peak[:, PEAKS:PEAKS + 1], ident[:, :], start=True, stop=True
                             ).then_inc(table_peak_ps_ready, 1)
            pe.wait_ge(scale_row_ready, 1)
            nc.tensor.matmul(caps_ps[:, P:P + 2], ones[0:1, :], scale_row[0:1, 0:2].bitcast(F32), start=True, stop=True
                             ).then_inc(scale_ps_ready, 1)
            for c in range(CHUNKS):
                pe.wait_ge(weight_ready, c + 1)
                if c == 0:
                    pe.wait_ge(ident16_ready, 1)
                for blk in range(BLOCKS):
                    pe.wait_ge(high_ready, c * BLOCKS + blk + 1)
                    pe.wait_ge(low_ready, c * BLOCKS + blk + 1)
                    for t in range(blk * BLOCK, (blk + 1) * BLOCK):
                        cols = slice(t * HALVES, (t + 1) * HALVES)
                        for part in range(PARTS):
                            last = nc.tensor.matmul(acc[:, cols], split[:, t, part, :], weight_kb[:, c, cols],
                                                    start=(part == 0), stop=(part == PARTS - 1))
                    if blk == BLOCKS - 1:
                        last.then_inc(acc_ready, 1)
                    for q in range(blk * BLOCK // FILL, (blk + 1) * BLOCK // FILL):
                        fill(fill_at[("items", c, q)])
                    if c >= 1 and blk == 0:
                        pe.wait_ge(match_in_ready, c)
                        nc.tensor.matmul(norm[:, :], ones[:, :], factor[:, :], start=True, stop=True
                                         ).then_inc(match_ready, 1)
                pe.wait_ge(newest_in, 16 * (c + 1))
                if c == 0:
                    pe.wait_ge(weight_ready, CHUNKS)
                else:
                    pe.wait_ge(match_shifted, c)
                if c == 0:
                    pe.wait_ge(overflow_ready, 1)
                    nc.tensor.matmul(lists[0:1, P:P + 1], ones[:, 0:1], overflow_any[:, 0:1], start=True, stop=True
                                     ).then_inc(overflow_ps_ready, 1)
                nc.tensor.transpose(lists[:, 0:P], newest[:, :], ident[:, :]).then_inc(newestT_ps_ready, 1)
                gap = iter(range(UNITS))
                for i in range(STEPS):
                    v = c * STEPS + i
                    if i > 0:
                        pe.wait_ge(coef_ready, c * (STEPS - 1) + i)
                        tile_products(split, coef_parts, coef_low).then_inc(acc_ready, 1)
                    pe.wait_ge(sums_ready, v + 1)
                    if c == 0 and i == 0:
                        pe.wait_ge(w_scaled, 1)
                    for k in range(K):
                        dst, wk = by_k(caps_ps[:, :], k), slice(k * D, (k + 1) * D)
                        nc.tensor.matmul(dst, w[:, wk], sums[:, 0:PAIRS] if i == 0 else by_k(sums[:, :], k),
                                         start=True, stop=False)
                        nc.tensor.matmul(dst, bias_all[:, wk], weight_k[:, c, :] if i == 0 else by_k(coef, k),
                                         start=False, stop=False)
                        last = nc.tensor.matmul(dst, masked_u[0:1, wk], masked_k[0:1, c, :], start=False, stop=True)
                    last.then_inc(caps_ps_ready, 1)
                    pe.wait_ge(squares_ready, v + 1)
                    if i == 0:
                        pe.wait_ge(newestT_ready, c + 1)
                        pe.wait_ge(flag_ready, 1)
                    nc.tensor.matmul(norm[:, :], ones[:, :], squares[:, :], start=True, stop=True
                                     ).then_inc(norm_ready, 1)
                    if c >= 1:
                        for _ in range(GAPS[2 * i]):
                            score_unit(c - 1, next(gap))
                    if i < STEPS - 1:
                        pe.wait_ge(caps_ready, c * (STEPS - 1) + i + 1)
                        for k in range(K):
                            last = nc.tensor.matmul(by_k(acc[:, 0:COLS], k), wT[:, k * D:(k + 1) * D],
                                                    by_k(caps_sum[:, :], k),
                                                    start=True, stop=True)
                        last.then_inc(proj_ps_ready, 1)
                        if c == 0 and i == 0:
                            pe.wait_ge(bias_rep_ready, 1)
                        for k in range(K):
                            nc.tensor.matmul(by_k(caps_ps[:, :], k), bias_rep[:, k, :], by_k(caps_sum[:, :], k),
                                             start=True, stop=True)
                        pe.wait_ge(proj_ready, c * (STEPS - 1) + i + 1)
                        if i == 0:
                            for engine, done in trans_read.items():
                                pe.wait_ge(done, reads(engine, fill_at[("items", c, TILES // FILL - 1)]))
                        tile_products(splitT, proj_parts, proj_low).then_inc(logits_ready, 1)
                        if c >= 1:
                            for _ in range(GAPS[2 * i + 1]):
                                score_unit(c - 1, next(gap))
            pe.wait_ge(match_in_ready, CHUNKS)
            nc.tensor.matmul(norm[:, :], ones[:, :], factor[:, :], start=True, stop=True
                             ).then_inc(match_ready, 1)
            for j in range(UNITS):
                score_unit(CHUNKS - 1, j)

            with wanted(pe):
                main_path_over(pe)
                for c in range(CHUNKS):
                    pe.wait_ge(g_listed, c + 1)
                    if c >= 1:
                        pe.wait_ge(g_lists_read, c)
                    for i, part in enumerate((slice(0, P), slice(P, SEQ))):
                        count = part.stop - part.start
                        nc.tensor.transpose(lists[0:count, i * P:(i + 1) * P], eff[:, part], ident[:, :])
                        last = nc.tensor.transpose(lists[0:count, (2 + i) * P:(3 + i) * P], is_masked[:, part],
                                                   ident[:, :])
                    last.then_inc(g_listed_ps, 1)

                with pe.Fori(0, BATCH) as n:
                    pe.wait_ge(g_gathered, n * (16 * HALF) + 16 * HALF)
                    for i in range(HALF):
                        last = nc.tensor.transpose(trans[0][:, i * P:(i + 1) * P], g_rows[:, i * D:(i + 1) * D],
                                                   ident[:, :])
                    last.then_inc(g_trans_ready, 1)
                    for i in range(STEPS):
                        pe.wait_ge(g_coef_ready, n * STEPS + (i + 1))
                        for t in range(HALF):
                            last = nc.tensor.matmul(acc[:, 0:K], g_rows[:, t * D:(t + 1) * D], g_coef[:, t, :],
                                                    start=(t == 0), stop=(t == HALF - 1))
                        last.then_inc(g_acc_ready, 1)
                        pe.wait_ge(g_sums_ready, n * STEPS + (i + 1))
                        for k in range(K):
                            nc.tensor.matmul(caps_ps[:, k:k + 1], w[:, k * D:(k + 1) * D], sums[:, k:k + 1],
                                             start=True, stop=False)
                            for t in range(HALF):
                                last = nc.tensor.matmul(caps_ps[:, k:k + 1], bias_all[:, k * D:(k + 1) * D],
                                                        g_coef[:, t, k:k + 1], start=False, stop=(t == HALF - 1))
                        last.then_inc(g_caps_ps_ready, 1)
                        pe.wait_ge(g_squares_ready, n * STEPS + (i + 1))
                        nc.tensor.matmul(norm[:, 0:K], ones[:, :], squares[:, 0:K], start=True, stop=True
                                         ).then_inc(g_norm_ready, 1)
                        if i == STEPS - 1:
                            break
                        pe.wait_ge(g_caps_ready, n * (STEPS - 1) + (i + 1))
                        for k in range(K):
                            last = nc.tensor.matmul(acc[:, 8 + k:9 + k], wT[:, k * D:(k + 1) * D],
                                                    caps_sum[:, k:k + 1], start=True, stop=True)
                        last.then_inc(g_proj_ps_ready, 1)
                        pe.wait_ge(g_proj_ready, n * (STEPS - 1) + (i + 1))
                        if i == 0:
                            pe.wait_ge(g_rowsT_ready, n + 1)
                        for t in range(HALF):
                            for k in range(K):
                                nc.tensor.matmul(g_logits[:, t, k:k + 1], bias_rep[:, k, :], caps_sum[:, k:k + 1],
                                                 start=(t == 0 and k == 0), stop=False, skip_group_check=True)
                            last = nc.tensor.matmul(g_logits[:, t, :], g_rowsT[:, t * P:(t + 1) * P], proj[:, 0:K],
                                                    start=False, stop=(t == HALF - 1), skip_group_check=True)
                        last.then_inc(g_logits_ready, 1)
                    pe.wait_ge(g_match_in_ready, n + 1)
                    nc.tensor.matmul(norm[:, 0:K], ones[:, :], factor[:, 0:K], start=True, stop=True
                                     ).then_inc(g_match_ready, 1)

                pe.wait_ge(g_final_ready, 1)
                for u in range(CHUNKS * UNITS):
                    c, j = divmod(u, UNITS)
                    if u >= 2:
                        pe.wait_ge(g_score_read, u - 1)
                    nc.tensor.matmul(score[u % 2][:, 0:UNIT], g_final[:, c * P:(c + 1) * P],
                                     tableT[:, j * UNIT:(j + 1) * UNIT], start=True, stop=True
                                     ).then_inc(g_score_ready, 1)


_INS = ["r_seq", "L0_rec_emb_table", "L0_rec_s_w", "L0_rec_s_b"]


def kernel(**inputs):
    import numpy as np
    import concourse.bacc as bacc
    from concourse.bass_utils import run_bass_kernel_spmd

    nc = bacc.Bacc("TRN2", target_bir_lowering=False, num_devices=1)
    arrays, args = {}, []
    for name in _INS:
        a = np.ascontiguousarray(inputs[name])
        arrays[f"in_{name}"] = a
        args.append(nc.dram_tensor(f"in_{name}", a.shape, mybir.dt.from_np(a.dtype), kind="ExternalInput").ap())
    shape = (inputs["r_seq"].shape[0], inputs["L0_rec_emb_table"].shape[0])
    args.append(nc.dram_tensor("scores", shape, F32, kind="ExternalOutput").ap())
    capsule_routing(nc, *args)
    result = run_bass_kernel_spmd(nc, [arrays], core_ids=[0])
    return result.results[0]["scores"]
```

```python
from contextlib import ExitStack

import concourse.bass as bass
from concourse import mybir

F32 = mybir.dt.float32
F16 = mybir.dt.float16
BF16 = mybir.dt.bfloat16
I32 = mybir.dt.int32
ALU = mybir.AluOpType
ACT = mybir.ActivationFunctionType
AX = mybir.AxisListType.X

P = 128
STEPS = 3


def capsule_routing(nc, r_seq, table, s_w, s_b, out):
    BATCH, SEQ = r_seq.shape
    ITEMS, D = table.shape
    K = s_w.shape[1] // D
    assert D == P and BATCH % P == 0 and s_b.shape[0] == K * D
    CHUNKS = BATCH // P
    SLOTS = 64
    HALVES = P // SLOTS
    TILES = P // HALVES
    PAIRS = TILES * HALVES
    COLS = PAIRS * K
    BLOCK = 8
    BLOCKS = TILES // BLOCK
    FILL = 4
    GONE = -30000.0
    EPS = 1e-12
    TINY = 1e-30

    GROUP = FILL * P
    GROUPS = -(-ITEMS // GROUP)
    STAGES = 8
    UNIT = 500
    UNITS = ITEMS // UNIT
    assert UNITS * UNIT == ITEMS
    STORE = 1
    STORES = UNITS // STORE
    RING = 3
    SLOTS_OUT = 4
    PARTS = 2
    PEAKS = 5
    COEF_SCALE = 256
    SCALES = 5
    assert SEQ * COEF_SCALE < 65504
    MIDDLE = {("caps", 0): 1, ("factor", 0): 1, ("proj", 0): 1, ("products", 0): 2, ("logits", 0): 5,
              ("caps", 1): 1, ("norm", 1): 2, ("factor", 1): 1, ("proj", 1): 1, ("logits", 1): 1, ("caps", 2): 1}
    LAST = {**MIDDLE, ("factor", 1): 2, ("products", 1): 2, ("logits", 1): 7, ("norm", 2): 2, ("factor", 2): 7}
    GAPS = [{}] + [MIDDLE] * (CHUNKS - 2) + [LAST]
    FIRST_SUMS = {("norm", 2): range(0, 5), ("factor", 2): range(5, 8)}
    FILLS = {("products", 1): 2, ("logits", 1): 4, ("caps", 2): 1, ("factor", 2): 3,
             ("caps", 0): 1, ("norm", 0): 2, ("factor", 0): 3}
    EARLY = 2
    LATE = {1: 2, 4: 3}
    SPLITS = [("norm", 0), ("proj", 0), ("logits", 0), ("sums", 1),
              ("norm", 1), ("proj", 1), ("logits", 1), ("sums", 2)]
    assert len(GAPS) == CHUNKS and STORES * STORE == UNITS
    assert all(sum(sum(g.values()) for g in GAPS[:c + 1]) <= c * UNITS for c in range(CHUNKS))

    def group_parts(g):
        return min(GROUP, ITEMS - g * GROUP) // FILL

    assert all(group_parts(g) * FILL == min(GROUP, ITEMS - g * GROUP) for g in range(GROUPS))

    fills = [("table", g) for g in range(GROUPS)]
    fills += [("items", c, q) for c in range(CHUNKS) for q in range(TILES // FILL)]
    fill_at = {f: n for n, f in enumerate(fills)}
    reader = ["dve" if f[0] == "items" and f[1] == 0 and f[2] % 2 == 1 else "act" for f in fills]

    def reads(engine, n):
        return reader[:n + 1].count(engine)

    ctx = ExitStack()
    with ctx:
        def sb(name, shape, dt=F32):
            return ctx.enter_context(nc.sbuf_tensor(name, shape, dt))

        def bank(name, banks=1):
            return ctx.enter_context(nc.psum_tensor(name, [P, banks * 512], F32))

        def sem(name):
            return ctx.enter_context(nc.semaphore(name))

        tableT = sb("tableT", [P, ITEMS])
        ring = sb("ring", [P, RING, BLOCK * D])
        split = sb("split", [P, 2, TILES, PARTS, D], F16)
        first_rows = split[:, 1, :, :, :].rearrange("p t i d -> p (t i d)").bitcast(F32)
        splitT = sb("splitT", [P, TILES, PARTS, P], F16)
        outst = sb("outst", [P, SLOTS_OUT, STORE * UNIT])
        stage = splitT[:, :, :, :].rearrange("p t i d -> p (t i d)").bitcast(F32)
        w = sb("w", [P, K * D])
        wT = sb("wT", [P, K * D])
        bias_col = sb("bias_col", [P, K])
        bias_all = sb("bias_all", [P, K * D])
        bias_rep = sb("bias_rep", [P, K, P])
        ident16 = sb("ident16", [P, P], F16)
        table_peak = sb("table_peak", [P, PEAKS])
        peaks = sb("peaks", [P, 2])
        scale_row = sb("scale_row", [1, SCALES + 2], I32)
        scale = sb("scale", [P, SCALES])
        row_scale, sums_scale, proj_scale, logits_scale, proj_unscale = (scale[:, i:i + 1] for i in range(SCALES))
        row0 = sb("row0", [P, 1])
        masked_u = sb("masked_u", [1, K * D])
        ident = sb("ident", [P, P])
        ones = sb("ones", [P, P])
        tiny = sb("tiny", [P, 1])
        seq = sb("seq", [P, CHUNKS, SEQ], I32)
        scratch = outst[:, :, :].rearrange("p m n -> p (m n)")
        raw, eff, is_masked, is_last, keys = (scratch[:, i * SEQ:(i + 1) * SEQ] for i in range(5))
        top = sb("top", [P, 1 + SLOTS])
        counts = sb("counts", [P, 2])
        slot_index = sb("slot_index", [P, HALVES, SLOTS])
        slot_weight = sb("slot_weight", [P, HALVES, SLOTS])
        overflow = sb("overflow", [P, CHUNKS])
        overflow_any = sb("overflow_any", [P, 1])
        flag = sb("flag", [1, 1], I32)
        index = sb("index", [P, CHUNKS, TILES], I32)
        weight = sb("weight", [P, CHUNKS, TILES, HALVES])
        weight_kb = sb("weight_kb", [P, CHUNKS, PAIRS], BF16)
        masked_k = sb("masked_k", [1, CHUNKS, PAIRS])
        newest_index = sb("newest_index", [P, CHUNKS], I32)
        newest = sb("newest", [P, D])
        newestT = sb("newestT", [P, P])
        sums = sb("sums", [P, COLS])
        squares = sb("squares", [P, COLS])
        bias_row = squares[0:1, :]
        coef = sb("coef", [P, COLS])
        parts = sb("parts", [P, PARTS, COLS], F16)
        caps = sb("caps", [P, COLS])
        caps_sum = sb("caps_sum", [P, COLS])
        length = squares
        expd = squares
        bias_logits = squares
        match_exp = sb("match_exp", [P, COLS])
        QUARTERS = COLS // P
        square_sum = sb("square_sum", [P, QUARTERS])
        norm_length = sb("norm_length", [P, QUARTERS])
        norm_factor = sb("norm_factor", [P, QUARTERS])
        s_copy = sums
        factor = sb("factor", [P, COLS])
        shifted = factor
        peak = sb("peak", [P, PAIRS])
        total = sb("total", [P, PAIRS])
        ratio = sb("ratio", [P, PAIRS])
        final = [sb(f"final{c}", [P, P]) for c in range(CHUNKS)]

        trans = [bank("trans0"), bank("trans1")]
        score = [bank("score0"), bank("score1")]
        acc = bank("acc", 2)
        caps_ps = bank("caps_ps")
        norm = bank("norm")
        lists = norm

        seq_in = sem("seq_in")
        params_in = sem("params_in")
        table_in = [sem(f"table_in{i}") for i in range(STAGES)]
        first_gathered = [sem(f"first_gathered{i}") for i in range(BLOCKS)]
        ring_gathered = [sem(f"ring_gathered{i}") for i in range(RING)]
        ident16_ready = sem("ident16_ready")
        table_peak_ready = sem("table_peak_ready")
        table_peak_ps_ready = sem("table_peak_ps_ready")
        scale_row_ready = sem("scale_row_ready")
        scale_ps_ready = sem("scale_ps_ready")
        scale_ready = sem("scale_ready")
        w_scaled = sem("w_scaled")
        high_ready = sem("high_ready")
        low_ready = sem("low_ready")
        newestT_ready = sem("newestT_ready")
        proj_copied = sem("proj_copied")
        newest_in = sem("newest_in")
        ident_ready = sem("ident_ready")
        zeroed = sem("zeroed")
        bias_rep_ready = sem("bias_rep_ready")
        ones_ready = sem("ones_ready")
        wT_ps_ready = sem("wT_ps_ready")
        bias_ps_ready = sem("bias_ps_ready")
        masked_ps_ready = sem("masked_ps_ready")
        setup_out = sem("setup_out")
        slots_ready = sem("slots_ready")
        slotsT_ready = sem("slotsT_ready")
        index_ready = sem("index_ready")
        newest_index_ready = sem("newest_index_ready")
        weight_ready = sem("weight_ready")
        trans_full = sem("trans_full")
        trans_read = {"act": sem("trans_read_act"), "dve": sem("trans_read_dve")}
        newestT_ps_ready = sem("newestT_ps_ready")
        acc_ready = sem("acc_ready")
        sums_ready = sem("sums_ready")
        caps_ps_ready = sem("caps_ps_ready")
        caps_read = sem("caps_read")
        caps_copied = sem("caps_copied")
        factor_ready = sem("factor_ready")
        factor_ps_ready = sem("factor_ps_ready")
        even_ready = sem("even_ready")
        bias_logits_ps_ready = sem("bias_logits_ps_ready")
        bias_logits_ready = sem("bias_logits_ready")
        squares_ready = sem("squares_ready")
        norm_ready = sem("norm_ready")
        ln_ready = sem("ln_ready")
        length_ready = sem("length_ready")
        caps_ready = sem("caps_ready")
        proj_ps_ready = sem("proj_ps_ready")
        proj_ready = sem("proj_ready")
        logits_ready = sem("logits_ready")
        shifted_ready = sem("shifted_ready")
        expd_ready = sem("expd_ready")
        coef_ready = sem("coef_ready")
        match_in_ready = sem("match_in_ready")
        match_ready = sem("match_ready")
        match_shifted = sem("match_shifted")
        match_expd = sem("match_expd")
        final_ready = sem("final_ready")
        score_ready = sem("score_ready")
        score_read = sem("score_read")
        stored = [sem(f"stored{i}") for i in range(SLOTS_OUT)]
        overflow_ready = sem("overflow_ready")
        overflow_ps_ready = sem("overflow_ps_ready")
        flag_ready = sem("flag_ready")
        dve_done = sem("dve_done")

        HALF = 2
        REST = SEQ - P
        words = splitT[:, :, :, :].rearrange("p t i d -> p (t i d)").bitcast(F32)
        g_index = words[:, 0:HALF * BATCH].bitcast(I32).rearrange("p (i n) -> p i n", i=HALF)
        g_named = words[:, HALF * BATCH:2 * HALF * BATCH].rearrange("p (i n) -> p i n", i=HALF)
        g_final = words[:, 2 * HALF * BATCH:(2 * HALF + 1) * BATCH]
        g_rows, g_rowsT = ring[:, 0, 0:HALF * D], ring[:, 1, 0:HALF * P]
        g_proj = coef[:, HALF * K:HALF * K + K]
        g_live = peak[:, 0:HALF]
        g_index_now = index[:, 0, 0:HALF]
        g_named_now = ratio[:, 64:64 + HALF]
        g_coef = coef[:, 0:HALF * K].rearrange("p (i k) -> p i k", k=K)
        g_exp = expd[:, 0:HALF * K].rearrange("p (i k) -> p i k", k=K)
        g_exponent = shifted[:, 0:HALF * K].rearrange("p (i k) -> p i k", k=K)
        g_logits = caps_ps[:, 8:8 + HALF * K].rearrange("p (i k) -> p i k", k=K)
        g_listed = sem("g_listed")
        g_listed_ps = sem("g_listed_ps")
        g_lists_read = sem("g_lists_read")
        g_picked = sem("g_picked")
        g_taken = sem("g_taken")
        g_gathered = sem("g_gathered")
        g_trans_ready = sem("g_trans_ready")
        g_rowsT_ready = sem("g_rowsT_ready")
        g_coef_ready = sem("g_coef_ready")
        g_acc_ready = sem("g_acc_ready")
        g_sums_ready = sem("g_sums_ready")
        g_caps_ps_ready = sem("g_caps_ps_ready")
        g_squares_ready = sem("g_squares_ready")
        g_norm_ready = sem("g_norm_ready")
        g_ln_ready = sem("g_ln_ready")
        g_length_ready = sem("g_length_ready")
        g_caps_ready = sem("g_caps_ready")
        g_proj_ps_ready = sem("g_proj_ps_ready")
        g_proj_ready = sem("g_proj_ready")
        g_logits_ready = sem("g_logits_ready")
        g_shifted_ready = sem("g_shifted_ready")
        g_expd_ready = sem("g_expd_ready")
        g_match_in_ready = sem("g_match_in_ready")
        g_match_ready = sem("g_match_ready")
        g_match_shifted = sem("g_match_shifted")
        g_match_expd = sem("g_match_expd")
        g_final_ready = sem("g_final_ready")
        g_score_ready = sem("g_score_ready")
        g_score_read = sem("g_score_read")
        g_stored = [sem(f"g_stored{i}") for i in range(SLOTS_OUT)]
        g_setup_done = sem("g_setup_done")
        g_dve_done = sem("g_dve_done")
        G_STEPS = 31

        def wanted(engine):
            engine.wait_ge(flag_ready, 1)
            return engine.If(engine.value_load(flag[0:1, 0:1], min_val=0, max_val=1) != 0)

        def main_path_over(engine):
            for i in range(SLOTS_OUT):
                engine.wait_ge(stored[i], 16 * (CHUNKS * STORES // SLOTS_OUT))

        def by_k(t, k):
            return t.rearrange("p (n k) -> p n k", k=K)[:, :, k]

        def each_k(t):
            return t.rearrange("p (n k) -> p n k", k=K)

        def over_k(t):
            return t.unsqueeze(2).to_broadcast([P, PAIRS, K])

        HK = HALVES * K
        acc_parts = acc[:, :].rearrange("p (t i c) -> p t i c", i=2, c=HK)
        acc_sides = acc[:, :].rearrange("p (t i c) -> p t c i", i=2, c=HK)

        def by_tile(t):
            return t.rearrange("p (t c) -> p t c", c=HK)

        def gathered(b):
            if b < BLOCKS:
                place, done, uses = first_rows[:, b * BLOCK * D:(b + 1) * BLOCK * D], first_gathered[b], 1
            else:
                uses, slot = divmod(b - BLOCKS, RING)
                place, done, uses = ring[:, slot, :], ring_gathered[slot], uses + 1
            return place.rearrange("p (t d) -> p t d", d=D), done, 16 * BLOCK * uses

        def own_fills(wait):
            at = sum(n for (_, i), n in FILLS.items() if i > 0)
            for other, n in FILLS.items():
                if other[1] == 0:
                    if other == wait:
                        return range(at, at + n)
                    at += n
            return range(0)

        def block_part(b, part):
            c, blk = divmod(b, BLOCKS)
            return split[:, c % 2, blk * BLOCK:(blk + 1) * BLOCK, part, :]

        assert len(SPLITS) == BLOCKS and sum(FILLS.values()) == TILES // FILL
        assert BLOCK // FILL == 2

        block = ctx.enter_context(nc.Block())

        @block.sync
        def _(sp):
            sp.dma_start(seq[:, :, :], r_seq.rearrange("(c p) s -> p c s", p=P)).then_inc(seq_in, 16)
            sp.dma_start(w[:, :], s_w).then_inc(params_in, 16)
            sp.dma_start(bias_row, s_b.unsqueeze(0)).then_inc(params_in, 16)
            sp.dma_start(bias_col[:, :], s_b.rearrange("(k e) -> e k", k=K),
                         allow_slow_non_contiguous=True).then_inc(params_in, 16)
            sp.dma_start(row0[:, :], table[0:1, :].rearrange("o d -> d o"),
                         allow_slow_non_contiguous=True).then_inc(params_in, 16)
            for g in range(GROUPS):
                parts, s = group_parts(g), g % STAGES
                if g >= STAGES:
                    sp.wait_ge(trans_full, fill_at[("table", g - STAGES)] + 1)
                sp.dma_start(stage[0:parts, s * GROUP:(s + 1) * GROUP],
                             table[g * GROUP:g * GROUP + parts * FILL, :].rearrange("(p j) d -> p (j d)", j=FILL)
                             ).then_inc(table_in[s], 16)
            for m in range(CHUNKS * STORES):
                c, part = divmod(m, STORES)
                sp.wait_ge(score_read, (m + 1) * STORE)
                sp.dma_start(out[c * P:(c + 1) * P, part * STORE * UNIT:(part + 1) * STORE * UNIT],
                             outst[:, m % SLOTS_OUT, :]).then_inc(stored[m % SLOTS_OUT], 16)
            main_path_over(sp)

            with wanted(sp):
                for m in range(CHUNKS * STORES):
                    c, part = divmod(m, STORES)
                    sp.wait_ge(g_score_read, (m + 1) * STORE)
                    sp.dma_start(out[c * P:(c + 1) * P, part * STORE * UNIT:(part + 1) * STORE * UNIT],
                                 outst[:, m % SLOTS_OUT, :]).then_inc(g_stored[m % SLOTS_OUT], 16)
                for i in range(SLOTS_OUT):
                    sp.wait_ge(g_stored[i], 16 * (CHUNKS * STORES // SLOTS_OUT))

        @block.gpsimd
        def _(pool):
            nc.gpsimd.memset(ident[:, :], 0.0).then_inc(zeroed, 1)
            nc.gpsimd.memset(weight[:, :, :, :], 0.0).then_inc(zeroed, 1)
            pool.wait_ge(zeroed, 1)
            nc.gpsimd.affine_select(out=ident[:, :], in_=ident[:, :], compare_op=ALU.not_equal, fill=1.0, base=0,
                                    pattern=[[-1, P]], channel_multiplier=1).then_inc(ident_ready, 1)
            pool.wait_ge(ident_ready, 1)
            nc.gpsimd.tensor_copy(ident16[:, :], ident[:, :]).then_inc(ident16_ready, 1)
            pool.wait_ge(params_in, 64)
            nc.gpsimd.tensor_copy(bias_rep[:, :, :], bias_col[:, :].unsqueeze(2).to_broadcast([P, K, P])
                                  ).then_inc(bias_rep_ready, 1)
            for c in range(CHUNKS):
                pool.wait_ge(index_ready, c + 1)
                for b in range(c * BLOCKS, (c + 1) * BLOCKS):
                    if b >= BLOCKS + RING:
                        pool.wait_ge(high_ready, b - RING + 1)
                        pool.wait_ge(low_ready, b - RING + 1)
                    place, done, _ = gathered(b)
                    for t in range(BLOCK):
                        at = b % BLOCKS * BLOCK + t
                        nc.gpsimd.indirect_dma_start(
                            out=place[:, t, :], out_offset=None, in_=table,
                            in_offset=bass.IndirectOffsetOnAxis(ap=index[:, c, at:at + 1], axis=0)
                        ).then_inc(done, 16)
                pool.wait_ge(newest_index_ready, c + 1)
                if c >= 1:
                    pool.wait_ge(newestT_ps_ready, c)
                nc.gpsimd.indirect_dma_start(
                    out=newest[:, :], out_offset=None, in_=table,
                    in_offset=bass.IndirectOffsetOnAxis(ap=newest_index[:, c:c + 1], axis=0)
                ).then_inc(newest_in, 16)

            with wanted(pool):
                main_path_over(pool)
                with pool.Fori(0, BATCH) as n:
                    pool.wait_ge(g_picked, n + 1)
                    pool.sem_inc(g_taken, 1)
                    for i in range(HALF):
                        nc.gpsimd.indirect_dma_start(
                            out=g_rows[:, i * D:(i + 1) * D], out_offset=None, in_=table,
                            in_offset=bass.IndirectOffsetOnAxis(ap=g_index_now[:, i:i + 1], axis=0)
                        ).then_inc(g_gathered, 16)

        @block.scalar
        def _(act):
            def fill_out(n):
                act.wait_ge(trans_full, n + 1)
                f = fills[n]
                src = trans[n % 2]
                if f[0] == "table":
                    m = FILL * group_parts(f[1])
                    nc.scalar.copy(tableT[:, f[1] * GROUP:f[1] * GROUP + m].rearrange("d (p j) -> d j p", j=FILL),
                                   src[:, 0:m].rearrange("d (j p) -> d j p", j=FILL)).then_inc(trans_read["act"], 1)
                else:
                    nc.scalar.copy(splitT[:, f[2] * FILL:(f[2] + 1) * FILL, :, :].rearrange("p t i s -> p (t i s)"),
                                   src[:, :].bitcast(F16)).then_inc(trans_read["act"], 1)

            def score_out(u):
                j, m = u % UNITS, u // STORE
                act.wait_ge(score_ready, u + 1)
                if j % STORE == 0 and m >= SLOTS_OUT:
                    act.wait_ge(stored[m % SLOTS_OUT], 16 * (m // SLOTS_OUT))
                nc.scalar.copy(outst[:, m % SLOTS_OUT, (j % STORE) * UNIT:(j % STORE + 1) * UNIT],
                               score[u % 2][:, 0:UNIT]).then_inc(score_read, 1)

            def exp_match(c):
                act.wait_ge(match_shifted, c + 1)
                nc.scalar.activation(match_exp[:, :], shifted[:, :], ACT.Exp).then_inc(match_expd, 1)

            act.add_instruction(mybir.InstLoadActFuncSet(name=nc.get_next_instruction_name(), act_func_set_id=6))
            act.wait_ge(wT_ps_ready, 1)
            nc.scalar.copy(wT[:, :], score[0][:, :]).then_inc(setup_out, 1)
            act.wait_ge(bias_ps_ready, 1)
            nc.scalar.activation(bias_all[:, :], score[1][:, :], ACT.Copy, scale=1.0 / COEF_SCALE).then_inc(setup_out, 1)
            act.wait_ge(masked_ps_ready, 1)
            nc.scalar.copy(masked_u[:, :], norm[0:1, :]).then_inc(setup_out, 1)
            for g in range(GROUPS):
                fill_out(g)
            act.wait_ge(scale_ready, 1)
            def high(b):
                place, done, count = gathered(b)
                act.wait_ge(done, count)
                if b >= BLOCKS and b < 2 * BLOCKS:
                    act.wait_ge(low_ready, b - BLOCKS + 1)
                if b >= 2 * BLOCKS and b % BLOCKS == 0:
                    act.wait_ge(acc_ready, STEPS * (b // BLOCKS - 1))
                nc.scalar.activation(block_part(b, 0), place, ACT.Copy, scale=row_scale).then_inc(high_ready, 1)

            for b in range(BLOCKS):
                high(b)
                if b >= 1:
                    fill_out(fill_at[("items", 0, 2 * (b - 1))])
            unit = iter(range(CHUNKS * UNITS))
            for c in range(CHUNKS):
                next_fill = iter(range(TILES // FILL))

                def in_wait(wait):
                    if c + 1 < CHUNKS and wait in SPLITS:
                        high((c + 1) * BLOCKS + SPLITS.index(wait))
                    for _ in range(FILLS.get(wait, 0) if c + 1 < CHUNKS and wait[1] > 0 else 0):
                        fill_out(fill_at[("items", c + 1, next(next_fill))])
                    if wait[1] == 0 and c >= 1:
                        for q in own_fills(wait):
                            fill_out(fill_at[("items", c, q)])
                    for _ in range(GAPS[c].get(wait, 0)):
                        score_out(next(unit))

                for i in range(STEPS):
                    v = c * STEPS + i
                    if i == 0:
                        act.wait_ge(acc_ready, v + 1)
                        if c >= 1:
                            act.wait_ge(caps_read, c)
                        nc.scalar.copy(sums[:, 0:PAIRS], acc[:, 0:PAIRS]).then_inc(sums_ready, 1)
                        if c >= 1:
                            exp_match(c - 1)
                    else:
                        in_wait(("sums", i))
                    act.wait_ge(caps_ps_ready, v + 1)
                    nc.scalar.activation(squares[:, :], caps_ps[:, :], ACT.Square).then_inc(squares_ready, 1)
                    nc.scalar.copy(s_copy[:, :], caps_ps[:, :]).then_inc(caps_copied, 1)
                    in_wait(("caps", i))
                    act.wait_ge(norm_ready, v + 1)
                    nc.scalar.activation(norm_length[:, :], norm[:, 0:QUARTERS], ACT.Ln, bias=tiny[:, 0:1]
                                         ).then_inc(ln_ready, 1)
                    act.wait_ge(ln_ready, v + 1)
                    nc.scalar.activation(norm_length[:, :], norm_length[:, :], ACT.Exp, scale=0.5
                                         ).then_inc(length_ready, 1)
                    if c == 0 and i == 0:
                        fill_out(fill_at[("items", 0, 2 * (BLOCKS - 1))])
                    in_wait(("norm", i))
                    in_wait(("factor", i))
                    if i < STEPS - 1:
                        v = c * (STEPS - 1) + i
                        act.wait_ge(proj_ps_ready, v + 1)
                        nc.scalar.copy(parts[:, 0, :], acc[:, 0:COLS]).then_inc(proj_copied, 1)
                        act.wait_ge(bias_logits_ps_ready, v + 1)
                        nc.scalar.copy(bias_logits[:, :], caps_ps[:, :]).then_inc(bias_logits_ready, 1)
                        in_wait(("proj", i))
                        in_wait(("products", i))
                        act.wait_ge(shifted_ready, v + 1)
                        nc.scalar.activation(expd[:, :], shifted[:, :], ACT.Exp).then_inc(expd_ready, 1)
                        in_wait(("logits", i))
            exp_match(CHUNKS - 1)
            for u in unit:
                score_out(u)

            with wanted(act):
                main_path_over(act)
                with act.Fori(0, BATCH) as n:
                    act.wait_ge(g_trans_ready, n + 1)
                    nc.scalar.copy(g_rowsT, trans[0][:, 0:HALF * P]).then_inc(g_rowsT_ready, 1)
                    for i in range(STEPS):
                        act.wait_ge(g_acc_ready, n * STEPS + (i + 1))
                        nc.scalar.copy(sums[:, 0:K], acc[:, 0:K]).then_inc(g_sums_ready, 1)
                        act.wait_ge(g_caps_ps_ready, n * STEPS + (i + 1))
                        nc.scalar.activation(squares[:, 0:K], caps_ps[:, 0:K], ACT.Square).then_inc(g_squares_ready, 1)
                        act.wait_ge(g_norm_ready, n * STEPS + (i + 1))
                        nc.scalar.activation(length[:, 0:K], norm[:, 0:K], ACT.Ln, bias=tiny[:, 0:1]
                                             ).then_inc(g_ln_ready, 1)
                        act.wait_ge(g_ln_ready, n * STEPS + (i + 1))
                        nc.scalar.activation(length[:, 0:K], length[:, 0:K], ACT.Exp, scale=0.5
                                             ).then_inc(g_length_ready, 1)
                        if i < STEPS - 1:
                            act.wait_ge(g_proj_ps_ready, n * (STEPS - 1) + (i + 1))
                            nc.scalar.copy(g_proj, acc[:, 8:8 + K]).then_inc(g_proj_ready, 1)
                            act.wait_ge(g_shifted_ready, n * (STEPS - 1) + (i + 1))
                            nc.scalar.activation(g_exp, g_exponent, ACT.Exp).then_inc(g_expd_ready, 1)
                    act.wait_ge(g_match_shifted, n + 1)
                    nc.scalar.activation(expd[:, 0:K], shifted[:, 0:K], ACT.Exp).then_inc(g_match_expd, 1)
                for u in range(CHUNKS * UNITS):
                    m = u // STORE
                    act.wait_ge(g_score_ready, u + 1)
                    if u % STORE == 0 and m >= SLOTS_OUT:
                        act.wait_ge(g_stored[m % SLOTS_OUT], 16 * (m // SLOTS_OUT))
                    nc.scalar.copy(outst[:, m % SLOTS_OUT, (u % STORE) * UNIT:(u % STORE + 1) * UNIT],
                                   score[u % 2][:, 0:UNIT]).then_inc(g_score_read, 1)

        @block.vector
        def _(dve):
            steps = [0]

            def then(ins):
                steps[0] += 1
                ins.then_inc(dve_done, 1)
                dve.wait_ge(dve_done, steps[0])

            def prepare(c):
                then(nc.vector.tensor_copy(raw, seq[:, c, :]))
                nc.vector.tensor_single_scalar(is_masked, raw, 0.0, ALU.is_equal)
                then(nc.vector.tensor_scalar(keys, raw, 0.0, float(ITEMS), ALU.is_lt, ALU.mult))
                then(nc.vector.tensor_tensor(eff, raw, keys, ALU.add))
                then(nc.vector.tensor_scalar(eff, eff, 0.0, float(ITEMS - 1), ALU.max, ALU.min))
                then(nc.vector.tensor_single_scalar(is_last, eff, float(ITEMS - 1), ALU.is_equal))
                nc.vector.tensor_copy(newest_index[:, c:c + 1], eff[:, SEQ - 1:SEQ]).then_inc(newest_index_ready, 1)
                nc.vector.reduce_sum(counts[:, 0:1], is_masked, axis=AX)
                then(nc.vector.reduce_sum(counts[:, 1:2], is_last, axis=AX))
                then(nc.vector.tensor_tensor(is_last, is_last, is_masked, ALU.add))
                then(nc.vector.scalar_tensor_tensor(keys, is_last, GONE, eff, ALU.mult, ALU.add))
                for r in range(SLOTS // 8):
                    eight = top[:, 1 + 8 * r:9 + 8 * r]
                    then(nc.vector.max(out=eight, in_=keys))
                    then(nc.vector.match_replace(out=keys, in_to_replace=eight, in_values=keys,
                                                 imm_value=GONE))
                nc.vector.tensor_single_scalar(overflow[:, c:c + 1], top[:, SLOTS:SLOTS + 1], 0.0, ALU.is_ge)
                for h in range(HALVES):
                    nc.vector.memset(slot_index[:, h, 0:1], float(ITEMS - 1))
                    nc.vector.tensor_scalar_max(slot_index[:, h, 1:SLOTS], top[:, 1:SLOTS], 0.0)
                    nc.vector.tensor_copy(slot_weight[:, h, 0:1], counts[:, 1:2])
                    last = nc.vector.tensor_single_scalar(slot_weight[:, h, 1:SLOTS], top[:, 1:SLOTS], 0.0, ALU.is_ge)
                last.then_inc(slots_ready, 1)
                dve.wait_ge(slotsT_ready, c + 1)
                if c == 0:
                    dve.wait_ge(zeroed, 2)
                for h in range(HALVES):
                    here = slice(h * SLOTS, (h + 1) * SLOTS)
                    last = nc.vector.tensor_copy(index[here, c, :], lists[here, h * TILES:(h + 1) * TILES])
                last.then_inc(index_ready, 1)
                for h in range(HALVES):
                    here = slice(h * SLOTS, (h + 1) * SLOTS)
                    last = nc.vector.tensor_scalar_mul(weight[here, c, :, h],
                                                       lists[here, P + h * TILES:P + (h + 1) * TILES],
                                                       float(COEF_SCALE))
                then(last)
                nc.vector.tensor_scalar_mul(weight_kb[:, c, :], weight[:, c, :, :].rearrange("p t h -> p (t h)"), 1.0 / K)
                nc.vector.tensor_scalar_mul(masked_k[0:1, c, :].rearrange("p (t h) -> p h t", h=HALVES),
                                            lists[0:1, 2 * P:3 * P].rearrange("p (h t) -> p h t", h=HALVES),
                                            1.0 / K).then_inc(weight_ready, 1)

            def squash(dst, v):
                dve.wait_ge(ln_ready, v + 1)
                nc.vector.tensor_copy(square_sum[:, :], norm[:, 0:QUARTERS])
                then(nc.vector.tensor_scalar_add(norm_factor[:, :], norm[:, 0:QUARTERS], 1.0))
                dve.wait_ge(length_ready, v + 1)
                then(nc.vector.scalar_tensor_tensor(norm_factor[:, :], norm_length[:, :], EPS, norm_factor[:, :],
                                                    ALU.add, ALU.mult))
                then(nc.vector.reciprocal(norm_factor[:, :], norm_factor[:, :]))
                nc.vector.tensor_tensor(norm_factor[:, :], square_sum[:, :], norm_factor[:, :], ALU.mult
                                        ).then_inc(factor_ready, 1)
                dve.wait_ge(factor_ps_ready, v + 1)
                dve.wait_ge(caps_copied, v + 1)
                return nc.vector.tensor_tensor(dst[:, :], s_copy[:, :], norm[:, :], ALU.mult)

            def shift(src):
                then(nc.vector.reduce_max(peak[:, :], each_k(src), axis=AX))
                return nc.vector.tensor_tensor(each_k(shifted[:, :]), each_k(src), over_k(peak[:, :]), ALU.subtract)

            def table_peak_of(m):
                size = ITEMS // PEAKS
                last_group = min(GROUPS - 1, ((m + 1) * size - 1) // GROUP)
                dve.wait_ge(trans_read["act"], reads("act", fill_at[("table", last_group)]))
                return nc.vector.tensor_reduce(out=table_peak[:, m:m + 1], in_=tableT[:, m * size:(m + 1) * size],
                                               axis=AX, op=ALU.max, apply_absolute_value=True)

            nc.vector.memset(tiny[:, :], TINY)
            nc.vector.memset(ones[:, :], 1.0).then_inc(ones_ready, 1)
            dve.wait_ge(seq_in, 16)
            for c in range(EARLY):
                prepare(c)
            for m in range(PEAKS):
                last = table_peak_of(m)
            then(last)
            nc.vector.reduce_max(peaks[:, 0:1], table_peak[:, :], axis=AX)
            dve.wait_ge(params_in, 64)
            nc.vector.tensor_reduce(out=peaks[:, 1:2], in_=w[:, :], axis=AX, op=ALU.max, apply_absolute_value=True
                                    ).then_inc(table_peak_ready, 1)
            dve.wait_ge(table_peak_ps_ready, 1)
            t_bits, w_bits = scale_row[0:1, SCALES:SCALES + 1], scale_row[0:1, SCALES + 1:SCALES + 2]
            both = scale_row[0:1, SCALES:SCALES + 2]
            then(nc.vector.reduce_max(both.bitcast(F32), caps_ps[0:1, 0:2 * P].rearrange("p (x n) -> p x n", x=2),
                                      axis=AX))
            then(nc.vector.tensor_single_scalar(both, both, 23, ALU.logical_shift_right))
            nc.vector.tensor_scalar_max(t_bits, t_bits, 64.0)
            then(nc.vector.tensor_scalar_max(w_bits, w_bits, 88.0))
            nc.vector.tensor_scalar(scale_row[0:1, 0:1], t_bits, -1.0, 268.0, ALU.mult, ALU.add)
            nc.vector.tensor_scalar_add(scale_row[0:1, 1:2], t_bits, -22.0)
            nc.vector.tensor_scalar(scale_row[0:1, 2:3], w_bits, -1.0, 264.0, ALU.mult, ALU.add)
            nc.vector.scalar_tensor_tensor(scale_row[0:1, 3:4], t_bits, -151.0, w_bits, ALU.add, ALU.add)
            then(nc.vector.tensor_scalar_add(scale_row[0:1, 4:5], w_bits, -10.0))
            nc.vector.tensor_single_scalar(scale_row[0:1, 0:SCALES], scale_row[0:1, 0:SCALES], 23,
                                           ALU.logical_shift_left).then_inc(scale_row_ready, 1)
            dve.wait_ge(scale_ps_ready, 1)
            nc.vector.tensor_copy(scale[:, :], caps_ps[:, 2 * P:2 * P + SCALES]).then_inc(scale_ready, 1)
            dve.wait_ge(scale_ready, 1)
            dve.wait_ge(setup_out, 3)
            nc.vector.tensor_scalar(w[:, :], w[:, :], sums_scale, None, ALU.mult)
            nc.vector.tensor_scalar(wT[:, :], wT[:, :], proj_scale, None, ALU.mult).then_inc(w_scaled, 1)

            def attend(c):
                dve.wait_ge(match_ready, c + 1)
                shift(norm[:, :]).then_inc(match_shifted, 1)
                dve.wait_ge(match_expd, c + 1)
                nc.vector.reduce_sum(total[:, :], each_k(match_exp[:, :]), axis=AX)
                then(nc.vector.tensor_tensor(factor[:, :], match_exp[:, :], caps[:, :], ALU.mult))
                nc.vector.reciprocal(ratio[:, :], total[:, :])
                then(nc.vector.reduce_sum(peak[:, :], each_k(factor[:, :]), axis=AX))
                nc.vector.tensor_tensor(final[c][:, :].rearrange("e (h t) -> e h t", h=HALVES),
                                        peak[:, :].rearrange("e (t h) -> e h t", h=HALVES),
                                        ratio[:, :].rearrange("e (t h) -> e h t", h=HALVES), ALU.mult
                                        ).then_inc(final_ready, 1)

            def fill_out(n):
                q = fills[n][2]
                dve.wait_ge(trans_full, n + 1)
                nc.vector.tensor_copy(splitT[:, q * FILL:(q + 1) * FILL, :, :].rearrange("p t i s -> p (t i s)"),
                                      trans[n % 2][:, :].bitcast(F16)).then_inc(trans_read["dve"], 1)

            def low(b):
                dve.wait_ge(high_ready, b + 1)
                nc.vector.scalar_tensor_tensor(block_part(b, 1), gathered(b)[0], row_scale, block_part(b, 0),
                                               ALU.mult, ALU.subtract).then_inc(low_ready, 1)

            def even_coef(c):
                nc.vector.tensor_scalar_mul(coef[:, 0:PAIRS], weight[:, c, :, :].rearrange("p t h -> p (t h)"), 1.0 / K
                                            ).then_inc(even_ready, 1)

            even_coef(0)
            for b in range(BLOCKS):
                low(b)
                if b >= 1:
                    fill_out(fill_at[("items", 0, 2 * b - 1)])
                if b in LATE:
                    prepare(LATE[b])
            nc.vector.reduce_max(overflow_any[:, :], overflow[:, :], axis=AX).then_inc(overflow_ready, 1)
            for c in range(CHUNKS):

                def in_wait(wait):
                    if c + 1 < CHUNKS and wait in SPLITS:
                        low((c + 1) * BLOCKS + SPLITS.index(wait))

                if c >= 1:
                    dve.wait_ge(caps_ps_ready, STEPS * c)
                    even_coef(c)
                if c >= 1:
                    attend(c - 1)
                for i in range(STEPS):
                    v = c * STEPS + i
                    if i > 0:
                        dve.wait_ge(acc_ready, v + 1)
                        nc.vector.reduce_sum(by_tile(sums[:, :]), acc_sides, axis=AX).then_inc(sums_ready, 1)
                        in_wait(("sums", i))
                    dve.wait_ge(norm_ready, v + 1)
                    if i == 0:
                        squash(caps_sum, v).then_inc(caps_ready, 1)
                        if c == 0:
                            fill_out(fill_at[("items", 0, 2 * BLOCKS - 1)])
                    elif i < STEPS - 1:
                        then(squash(caps, v))
                        nc.vector.tensor_tensor(caps_sum[:, :], caps_sum[:, :], caps[:, :], ALU.add
                                                ).then_inc(caps_ready, 1)
                    else:
                        squash(caps, v).then_inc(caps_read, 1)
                        dve.wait_ge(caps_read, c + 1)
                    if i < STEPS - 1:
                        x = c * (STEPS - 1) + i + 1
                        in_wait(("norm", i))
                        dve.wait_ge(proj_copied, x)
                        nc.vector.tensor_tensor(parts[:, 1, :], acc[:, 0:COLS], parts[:, 0, :], ALU.subtract
                                                ).then_inc(proj_ready, 1)
                        if i == 0:
                            dve.wait_ge(newestT_ps_ready, c + 1)
                            nc.vector.tensor_copy(newestT[:, :].rearrange("d (t h) -> d h t", h=HALVES),
                                                  lists[:, 0:P].rearrange("d (h t) -> d h t", h=HALVES)
                                                  ).then_inc(newestT_ready, 1)
                        if c == 0 and i == 0:
                            dve.wait_ge(overflow_ps_ready, 1)
                            nc.vector.tensor_scalar_min(flag[:, :], lists[0:1, P:P + 1], 1.0).then_inc(flag_ready, 1)
                        in_wait(("proj", i))
                        dve.wait_ge(logits_ready, x)
                        dve.wait_ge(bias_logits_ready, x)
                        then(nc.vector.scalar_tensor_tensor(by_tile(shifted[:, :]), acc_parts[:, :, 0, :],
                                                            logits_scale, by_tile(bias_logits[:, :]),
                                                            ALU.mult, ALU.add))
                        then(nc.vector.scalar_tensor_tensor(by_tile(shifted[:, :]), acc_parts[:, :, 1, :],
                                                            logits_scale, by_tile(shifted[:, :]),
                                                            ALU.mult, ALU.add))
                        shift(shifted[:, :]).then_inc(shifted_ready, 1)
                        dve.wait_ge(expd_ready, x)
                        then(nc.vector.reduce_sum(total[:, :], each_k(expd[:, :]), axis=AX))
                        then(nc.vector.reciprocal(ratio[:, :], total[:, :]))
                        then(nc.vector.tensor_tensor(ratio[:, :], ratio[:, :],
                                                     weight[:, c, :, :].rearrange("p t h -> p (t h)"), ALU.mult))
                        then(nc.vector.tensor_tensor(each_k(coef[:, :]), each_k(expd[:, :]), over_k(ratio[:, :]),
                                                     ALU.mult))
                        then(nc.vector.tensor_copy(parts[:, 0, :], coef[:, :]))
                        nc.vector.tensor_tensor(parts[:, 1, :], coef[:, :], parts[:, 0, :], ALU.subtract
                                                ).then_inc(coef_ready, 1)
                        in_wait(("logits", i))
                nc.vector.tensor_tensor(each_k(factor[:, :]), each_k(caps[:, :]), over_k(newestT[:, :]), ALU.mult
                                        ).then_inc(match_in_ready, 1)
            attend(CHUNKS - 1)

            with wanted(dve):
                main_path_over(dve)
                setup = [0]

                def settle(ins):
                    setup[0] += 1
                    ins.then_inc(g_setup_done, 1)
                    dve.wait_ge(g_setup_done, setup[0])

                nc.vector.memset(g_live, 0.0)
                nc.vector.memset(g_index, 0)
                nc.vector.tensor_scalar(w[:, :], w[:, :], row_scale, float(COEF_SCALE), ALU.mult, ALU.mult)
                nc.vector.tensor_scalar(wT[:, :], wT[:, :], proj_unscale, None, ALU.mult)
                nc.vector.tensor_scalar_mul(bias_all[:, :], bias_all[:, :], float(COEF_SCALE))
                settle(nc.vector.memset(g_named, 1.0))
                nc.vector.memset(g_live[:, 0:1], 1.0)
                settle(nc.vector.memset(g_live[0:REST, 1:2], 1.0))
                for c in range(CHUNKS):
                    settle(nc.vector.tensor_copy(raw, seq[:, c, :]))
                    nc.vector.tensor_single_scalar(is_masked, raw, 0.0, ALU.not_equal)
                    settle(nc.vector.tensor_scalar(keys, raw, 0.0, float(ITEMS), ALU.is_lt, ALU.mult))
                    settle(nc.vector.tensor_tensor(eff, raw, keys, ALU.add))
                    nc.vector.tensor_scalar(eff, eff, 0.0, float(ITEMS - 1), ALU.max, ALU.min).then_inc(g_listed, 1)
                    dve.wait_ge(g_listed_ps, c + 1)
                    for i, count in enumerate((P, REST)):
                        nc.vector.tensor_copy(g_index[0:count, i, c * P:(c + 1) * P],
                                              lists[0:count, i * P:(i + 1) * P])
                        last = nc.vector.tensor_copy(g_named[0:count, i, c * P:(c + 1) * P],
                                                     lists[0:count, (2 + i) * P:(3 + i) * P])
                    last.then_inc(g_lists_read, 1)
                    dve.wait_ge(g_lists_read, c + 1)

                with dve.Fori(0, BATCH) as n:
                    done = [0]

                    def then_(ins):
                        done[0] += 1
                        ins.then_inc(g_dve_done, 1)
                        dve.wait_ge(g_dve_done, n * G_STEPS + done[0])

                    def over_tiles(t):
                        return t.unsqueeze(2).to_broadcast([P, HALF, K])

                    nc.vector.tensor_copy(g_index_now, g_index[:, :, bass.ds(n, 1)].rearrange("p i o -> p (i o)")
                                          ).then_inc(g_picked, 1)
                    then_(nc.vector.tensor_copy(g_named_now,
                                                g_named[:, :, bass.ds(n, 1)].rearrange("p i o -> p (i o)")))
                    nc.vector.tensor_scalar_mul(g_coef, over_tiles(g_live), 1.0 / K).then_inc(g_coef_ready, 1)
                    for i in range(STEPS):
                        dve.wait_ge(g_ln_ready, n * STEPS + (i + 1))
                        then_(nc.vector.tensor_scalar_add(factor[:, 0:K], norm[:, 0:K], 1.0))
                        dve.wait_ge(g_length_ready, n * STEPS + (i + 1))
                        then_(nc.vector.scalar_tensor_tensor(factor[:, 0:K], length[:, 0:K], EPS, factor[:, 0:K],
                                                             ALU.add, ALU.mult))
                        then_(nc.vector.reciprocal(factor[:, 0:K], factor[:, 0:K]))
                        then_(nc.vector.tensor_tensor(factor[:, 0:K], norm[:, 0:K], factor[:, 0:K], ALU.mult))
                        if i == 0:
                            nc.vector.tensor_tensor(caps_sum[:, 0:K], caps_ps[:, 0:K], factor[:, 0:K], ALU.mult
                                                    ).then_inc(g_caps_ready, 1)
                        else:
                            then_(nc.vector.tensor_tensor(caps[:, 0:K], caps_ps[:, 0:K], factor[:, 0:K], ALU.mult))
                        if i == STEPS - 1:
                            break
                        if i > 0:
                            nc.vector.tensor_tensor(caps_sum[:, 0:K], caps_sum[:, 0:K], caps[:, 0:K], ALU.add
                                                    ).then_inc(g_caps_ready, 1)
                        dve.wait_ge(g_logits_ready, n * (STEPS - 1) + (i + 1))
                        then_(nc.vector.tensor_tensor(g_exponent, g_logits, over_tiles(g_named_now), ALU.mult))
                        then_(nc.vector.reduce_max(total[:, 0:HALF], g_exponent, axis=AX))
                        nc.vector.tensor_tensor(g_exponent, g_exponent, over_tiles(total[:, 0:HALF]), ALU.subtract
                                                ).then_inc(g_shifted_ready, 1)
                        dve.wait_ge(g_expd_ready, n * (STEPS - 1) + (i + 1))
                        then_(nc.vector.reduce_sum(total[:, 0:HALF], g_exp, axis=AX))
                        then_(nc.vector.reciprocal(ratio[:, 0:HALF], total[:, 0:HALF]))
                        then_(nc.vector.tensor_tensor(ratio[:, 0:HALF], ratio[:, 0:HALF], g_live, ALU.mult))
                        nc.vector.tensor_tensor(g_coef, g_exp, over_tiles(ratio[:, 0:HALF]), ALU.mult
                                                ).then_inc(g_coef_ready, 1)
                    newest_row = g_rowsT[:, SEQ - 1:SEQ]
                    nc.vector.tensor_scalar(factor[:, 0:K], caps[:, 0:K], newest_row, None, ALU.mult
                                            ).then_inc(g_match_in_ready, 1)
                    dve.wait_ge(g_match_ready, n + 1)
                    then_(nc.vector.reduce_max(total[:, 0:1], norm[:, 0:K], axis=AX))
                    nc.vector.tensor_scalar(shifted[:, 0:K], norm[:, 0:K], total[:, 0:1], None, ALU.subtract
                                            ).then_inc(g_match_shifted, 1)
                    dve.wait_ge(g_match_expd, n + 1)
                    then_(nc.vector.reduce_sum(total[:, 0:1], expd[:, 0:K], axis=AX))
                    then_(nc.vector.tensor_tensor(factor[:, 0:K], expd[:, 0:K], caps[:, 0:K], ALU.mult))
                    then_(nc.vector.reciprocal(ratio[:, 0:1], total[:, 0:1]))
                    then_(nc.vector.reduce_sum(total[:, 1:2], factor[:, 0:K], axis=AX))
                    then_(nc.vector.tensor_tensor(g_final[:, bass.ds(n, 1)], total[:, 1:2], ratio[:, 0:1], ALU.mult))
                    assert done[0] == G_STEPS, done[0]
                nc.vector.tensor_copy(total[:, 0:1], total[:, 0:1]).then_inc(g_final_ready, 1)

        @block.tensor
        def _(pe):
            def fill(n):
                f = fills[n]
                if n >= 2:
                    pe.wait_ge(trans_read[reader[n - 2]], reads(reader[n - 2], n - 2))
                if f[0] == "table":
                    g, parts = f[1], group_parts(f[1])
                    pe.wait_ge(table_in[g % STAGES], 16 * (g // STAGES + 1))
                    for j in range(FILL):
                        at = (g % STAGES) * GROUP + j * D
                        last = nc.tensor.transpose(trans[n % 2][:, j * parts:(j + 1) * parts],
                                                   stage[0:parts, at:at + D], ident[0:parts, 0:parts])
                else:
                    pe.wait_ge(low_ready, f[1] * BLOCKS + f[2] * FILL // BLOCK + 1)
                    dst = trans[n % 2][:, :].bitcast(F16)
                    for j in range(FILL * PARTS):
                        last = nc.tensor.transpose(dst[:, j * P:(j + 1) * P],
                                                   split[:, f[1] % 2, f[2] * FILL + j // PARTS, j % PARTS, :],
                                                   ident16[:, :])
                last.then_inc(trans_full, 1)

            def slots_back(c):
                pe.wait_ge(slots_ready, c + 1)
                if c >= 1:
                    pe.wait_ge(weight_ready, c)
                nc.tensor.transpose(lists[:, 0:P], slot_index[:, :, :].rearrange("p h s -> p (h s)"), ident[:, :])
                nc.tensor.transpose(lists[:, P:2 * P], slot_weight[:, :, :].rearrange("p h s -> p (h s)"), ident[:, :])
                nc.tensor.matmul(lists[0:1, 2 * P:3 * P], counts[:, 0:1], ident[:, :], start=True, stop=True
                                 ).then_inc(slotsT_ready, 1)

            def score_unit(u):
                c, j = divmod(u, UNITS)
                if j == 0:
                    pe.wait_ge(final_ready, c + 1)
                if u == 0:
                    pe.wait_ge(trans_read["act"], GROUPS)
                if u >= 2:
                    pe.wait_ge(score_read, u - 1)
                nc.tensor.matmul(score[u % 2][:, 0:UNIT], final[c][:, :], tableT[:, j * UNIT:(j + 1) * UNIT],
                                 start=True, stop=True).then_inc(score_ready, 1)

            def masked_share(c):
                for k in range(K):
                    nc.tensor.matmul(by_k(caps_ps[:, :], k), masked_u[0:1, k * D:(k + 1) * D], masked_k[0:1, c, :],
                                     start=(k == 0), stop=False, skip_group_check=True)

            def bias_share(c, i):
                if i == 0:
                    pe.wait_ge(even_ready, c + 1)
                for k in range(K):
                    nc.tensor.matmul(by_k(caps_ps[:, :], k), bias_all[:, k * D:(k + 1) * D],
                                     coef[:, 0:PAIRS] if i == 0 else by_k(coef[:, :], k),
                                     start=False, stop=False, skip_group_check=True)

            def tile_products(lhs):
                for t in range(TILES):
                    here = slice(t * HK, (t + 1) * HK)
                    for side in range(PARTS):
                        last = nc.tensor.matmul(acc_parts[:, t, :, :], lhs[:, t, side, :], parts[:, :, here],
                                                start=(side == 0), stop=(side == PARTS - 1))
                return last

            pe.wait_ge(ident_ready, 1)
            pe.wait_ge(params_in, 64)
            pe.wait_ge(ones_ready, 1)
            for k in range(K):
                last = nc.tensor.transpose(score[0][:, k * P:(k + 1) * P], w[:, k * D:(k + 1) * D], ident[:, :])
            last.then_inc(wT_ps_ready, 1)
            nc.tensor.matmul(score[1][:, :], ones[0:1, :], bias_row, start=True, stop=True
                             ).then_inc(bias_ps_ready, 1)
            nc.tensor.matmul(norm[0:1, :], row0[:, 0:1], w[:, :], start=True, stop=False)
            nc.tensor.matmul(norm[0:1, :], ones[0:1, 0:1], bias_row, start=False, stop=True
                             ).then_inc(masked_ps_ready, 1)
            pe.wait_ge(setup_out, 3)
            slots_back(0)
            for g in range(GROUPS):
                fill(g)
                if g == 9:
                    slots_back(1)
            pe.wait_ge(table_peak_ready, 1)
            nc.tensor.matmul(caps_ps[0:1, 0:P], peaks[:, 0:1], ident[:, :], start=True, stop=True)
            nc.tensor.matmul(caps_ps[0:1, P:2 * P], peaks[:, 1:2], ident[:, :], start=True, stop=True
                             ).then_inc(table_peak_ps_ready, 1)
            pe.wait_ge(scale_row_ready, 1)
            nc.tensor.matmul(caps_ps[:, 2 * P:2 * P + SCALES], ones[0:1, :], scale_row[0:1, 0:SCALES].bitcast(F32),
                             start=True, stop=True).then_inc(scale_ps_ready, 1)

            def first_sums(b):
                c, blk = divmod(b, BLOCKS)
                if blk == 0:
                    pe.wait_ge(weight_ready, c + 1)
                pe.wait_ge(high_ready, b + 1)
                pe.wait_ge(low_ready, b + 1)
                for t in range(blk * BLOCK, (blk + 1) * BLOCK):
                    cols = slice(t * HALVES, (t + 1) * HALVES)
                    for part in range(PARTS):
                        last = nc.tensor.matmul(acc[:, cols], split[:, c % 2, t, part, :], weight_kb[:, c, cols],
                                                start=(part == 0), stop=(part == PARTS - 1))
                return last

            pe.wait_ge(ident16_ready, 1)
            for b in range(BLOCKS - 1):
                first_sums(b)
                for q in (2 * b, 2 * b + 1):
                    fill(fill_at[("items", 0, q)])
                if b in LATE:
                    slots_back(LATE[b])
            pe.wait_ge(scale_ready, 1)
            masked_share(0)
            bias_share(0, 0)
            first_sums(BLOCKS - 1).then_inc(acc_ready, 1)
            unit = iter(range(CHUNKS * UNITS))
            for c in range(CHUNKS):
                next_fill = iter(range(TILES // FILL))

                def in_wait(wait):
                    if c + 1 < CHUNKS and wait in FIRST_SUMS:
                        for blk in FIRST_SUMS[wait]:
                            last = first_sums((c + 1) * BLOCKS + blk)
                        if blk == BLOCKS - 1:
                            last.then_inc(acc_ready, 1)
                    for _ in range(FILLS.get(wait, 0) if c + 1 < CHUNKS and wait[1] > 0 else 0):
                        fill(fill_at[("items", c + 1, next(next_fill))])
                    if wait[1] == 0 and c >= 1:
                        for q in own_fills(wait):
                            fill(fill_at[("items", c, q)])
                    for _ in range(GAPS[c].get(wait, 0)):
                        score_unit(next(unit))

                if c == 0:
                    pe.wait_ge(weight_ready, CHUNKS)
                if c >= 1:
                    pe.wait_ge(caps_read, c)
                    masked_share(c)
                if c >= 1:
                    pe.wait_ge(match_in_ready, c)
                    nc.tensor.matmul(norm[:, :], ones[:, :], factor[:, :], start=True, stop=True
                                     ).then_inc(match_ready, 1)
                for i in range(STEPS):
                    v = c * STEPS + i
                    if i > 0:
                        pe.wait_ge(coef_ready, c * (STEPS - 1) + i)
                        tile_products(split[:, c % 2]).then_inc(acc_ready, 1)
                    if c >= 1 or i >= 1:
                        bias_share(c, i)
                    pe.wait_ge(sums_ready, v + 1)
                    if c == 0 and i == 0:
                        pe.wait_ge(w_scaled, 1)
                    for k in range(K):
                        last = nc.tensor.matmul(by_k(caps_ps[:, :], k), w[:, k * D:(k + 1) * D],
                                                sums[:, 0:PAIRS] if i == 0 else by_k(sums[:, :], k),
                                                start=False, stop=True, skip_group_check=True)
                    last.then_inc(caps_ps_ready, 1)
                    in_wait(("caps", i))
                    pe.wait_ge(squares_ready, v + 1)
                    if c >= 1 and i == 0:
                        pe.wait_ge(match_shifted, c)
                    if i == 1:
                        pe.wait_ge(newestT_ready, c + 1)
                        pe.wait_ge(flag_ready, 1)
                    for q in range(QUARTERS):
                        last = nc.tensor.matmul(norm[:, q:q + 1], squares[:, q * P:(q + 1) * P], ones[:, 0:1],
                                                start=True, stop=True)
                    last.then_inc(norm_ready, 1)
                    if c == 0 and i == 0:
                        for q in (2 * (BLOCKS - 1), 2 * BLOCKS - 1):
                            fill(fill_at[("items", 0, q)])
                    in_wait(("norm", i))
                    pe.wait_ge(factor_ready, v + 1)
                    for q in range(QUARTERS):
                        last = nc.tensor.matmul(norm[:, q * P:(q + 1) * P],
                                                norm_factor[:, q:q + 1].to_broadcast([P, P]), ident[:, :],
                                                start=True, stop=True)
                    last.then_inc(factor_ps_ready, 1)
                    in_wait(("factor", i))
                    if i < STEPS - 1:
                        pe.wait_ge(caps_ready, c * (STEPS - 1) + i + 1)
                        for k in range(K):
                            last = nc.tensor.matmul(by_k(acc[:, 0:COLS], k), wT[:, k * D:(k + 1) * D],
                                                    by_k(caps_sum[:, :], k),
                                                    start=True, stop=True)
                        last.then_inc(proj_ps_ready, 1)
                        if c == 0 and i == 0:
                            pe.wait_ge(bias_rep_ready, 1)
                        for k in range(K):
                            last = nc.tensor.matmul(by_k(caps_ps[:, :], k), bias_rep[:, k, :],
                                                    by_k(caps_sum[:, :], k), start=True, stop=True)
                        last.then_inc(bias_logits_ps_ready, 1)
                        if i == 0:
                            if c == 0:
                                pe.wait_ge(overflow_ready, 1)
                                nc.tensor.matmul(lists[0:1, P:P + 1], ones[:, 0:1], overflow_any[:, 0:1],
                                                 start=True, stop=True).then_inc(overflow_ps_ready, 1)
                            pe.wait_ge(newest_in, 16 * (c + 1))
                            nc.tensor.transpose(lists[:, 0:P], newest[:, :], ident[:, :]).then_inc(newestT_ps_ready, 1)
                        in_wait(("proj", i))
                        pe.wait_ge(proj_ready, c * (STEPS - 1) + i + 1)
                        if i == 0:
                            for engine, done in trans_read.items():
                                pe.wait_ge(done, reads(engine, fill_at[("items", c, TILES // FILL - 1)]))
                        tile_products(splitT).then_inc(logits_ready, 1)
                        in_wait(("products", i))
                        pe.wait_ge(bias_logits_ready, c * (STEPS - 1) + i + 1)
                        masked_share(c)
                        in_wait(("logits", i))
            pe.wait_ge(match_in_ready, CHUNKS)
            nc.tensor.matmul(norm[:, :], ones[:, :], factor[:, :], start=True, stop=True
                             ).then_inc(match_ready, 1)
            for u in unit:
                score_unit(u)

            with wanted(pe):
                main_path_over(pe)
                for c in range(CHUNKS):
                    pe.wait_ge(g_listed, c + 1)
                    if c >= 1:
                        pe.wait_ge(g_lists_read, c)
                    for i, part in enumerate((slice(0, P), slice(P, SEQ))):
                        count = part.stop - part.start
                        nc.tensor.transpose(lists[0:count, i * P:(i + 1) * P], eff[:, part], ident[:, :])
                        last = nc.tensor.transpose(lists[0:count, (2 + i) * P:(3 + i) * P], is_masked[:, part],
                                                   ident[:, :])
                    last.then_inc(g_listed_ps, 1)

                with pe.Fori(0, BATCH) as n:
                    pe.wait_ge(g_gathered, n * (16 * HALF) + 16 * HALF)
                    for i in range(HALF):
                        last = nc.tensor.transpose(trans[0][:, i * P:(i + 1) * P], g_rows[:, i * D:(i + 1) * D],
                                                   ident[:, :])
                    last.then_inc(g_trans_ready, 1)
                    for i in range(STEPS):
                        pe.wait_ge(g_coef_ready, n * STEPS + (i + 1))
                        for t in range(HALF):
                            last = nc.tensor.matmul(acc[:, 0:K], g_rows[:, t * D:(t + 1) * D], g_coef[:, t, :],
                                                    start=(t == 0), stop=(t == HALF - 1))
                        last.then_inc(g_acc_ready, 1)
                        pe.wait_ge(g_sums_ready, n * STEPS + (i + 1))
                        for k in range(K):
                            nc.tensor.matmul(caps_ps[:, k:k + 1], w[:, k * D:(k + 1) * D], sums[:, k:k + 1],
                                             start=True, stop=False)
                            for t in range(HALF):
                                last = nc.tensor.matmul(caps_ps[:, k:k + 1], bias_all[:, k * D:(k + 1) * D],
                                                        g_coef[:, t, k:k + 1], start=False, stop=(t == HALF - 1))
                        last.then_inc(g_caps_ps_ready, 1)
                        pe.wait_ge(g_squares_ready, n * STEPS + (i + 1))
                        nc.tensor.matmul(norm[:, 0:K], ones[:, :], squares[:, 0:K], start=True, stop=True
                                         ).then_inc(g_norm_ready, 1)
                        if i == STEPS - 1:
                            break
                        pe.wait_ge(g_caps_ready, n * (STEPS - 1) + (i + 1))
                        for k in range(K):
                            last = nc.tensor.matmul(acc[:, 8 + k:9 + k], wT[:, k * D:(k + 1) * D],
                                                    caps_sum[:, k:k + 1], start=True, stop=True)
                        last.then_inc(g_proj_ps_ready, 1)
                        pe.wait_ge(g_proj_ready, n * (STEPS - 1) + (i + 1))
                        if i == 0:
                            pe.wait_ge(g_rowsT_ready, n + 1)
                        for t in range(HALF):
                            for k in range(K):
                                nc.tensor.matmul(g_logits[:, t, k:k + 1], bias_rep[:, k, :], caps_sum[:, k:k + 1],
                                                 start=(t == 0 and k == 0), stop=False, skip_group_check=True)
                            last = nc.tensor.matmul(g_logits[:, t, :], g_rowsT[:, t * P:(t + 1) * P], g_proj,
                                                    start=False, stop=(t == HALF - 1), skip_group_check=True)
                        last.then_inc(g_logits_ready, 1)
                    pe.wait_ge(g_match_in_ready, n + 1)
                    nc.tensor.matmul(norm[:, 0:K], ones[:, :], factor[:, 0:K], start=True, stop=True
                                     ).then_inc(g_match_ready, 1)

                pe.wait_ge(g_final_ready, 1)
                for u in range(CHUNKS * UNITS):
                    c, j = divmod(u, UNITS)
                    if u >= 2:
                        pe.wait_ge(g_score_read, u - 1)
                    nc.tensor.matmul(score[u % 2][:, 0:UNIT], g_final[:, c * P:(c + 1) * P],
                                     tableT[:, j * UNIT:(j + 1) * UNIT], start=True, stop=True
                                     ).then_inc(g_score_ready, 1)


_INS = ["r_seq", "L0_rec_emb_table", "L0_rec_s_w", "L0_rec_s_b"]


def kernel(**inputs):
    import numpy as np
    import concourse.bacc as bacc
    from concourse.bass_utils import run_bass_kernel_spmd

    nc = bacc.Bacc("TRN2", target_bir_lowering=False, num_devices=1)
    arrays, args = {}, []
    for name in _INS:
        a = np.ascontiguousarray(inputs[name])
        arrays[f"in_{name}"] = a
        args.append(nc.dram_tensor(f"in_{name}", a.shape, mybir.dt.from_np(a.dtype), kind="ExternalInput").ap())
    shape = (inputs["r_seq"].shape[0], inputs["L0_rec_emb_table"].shape[0])
    args.append(nc.dram_tensor("scores", shape, F32, kind="ExternalOutput").ap())
    capsule_routing(nc, *args)
    result = run_bass_kernel_spmd(nc, [arrays], core_ids=[0])
    return result.results[0]["scores"]
```
